# Optimizing a Trainium2 kernel written in Bass

```python
import numpy as np
import jax
import jax.numpy as jnp

def _softmax(x, axis=-1):
    return jax.nn.softmax(x, axis=axis)

def _gelu(x):
    return jax.nn.gelu(x, approximate=True)

def _silu(x):
    return jax.nn.silu(x)

def _sigmoid(x):
    return jax.nn.sigmoid(x)

def _layernorm(x, axis=-1, eps=1e-05):
    m = jnp.mean(x, axis=axis, keepdims=True)
    v = jnp.var(x, axis=axis, keepdims=True)
    return (x - m) / jnp.sqrt(v + eps)

def _scatter_add(tgt, idx, src, axis=0):
    return tgt.at[idx].add(src)

def _segment_sum(src, seg, n):
    return jax.ops.segment_sum(src, seg, n)
kernel_name = 'mk_perceiver_d1_seqx_r8_4521a3'

def setup_inputs(seed: int=0):
    np.random.seed(seed)
    _w = jnp.asarray

    def _rec_inputs():
        import jax
        import jax.numpy as jnp
        _rk = jax.random.key(seed)
        x = -0.0005207 + 1.001 * jax.random.normal(jax.random.fold_in(_rk, 1), (1, 128, 512), jnp.float32)
        _lenS = 128 - jax.random.randint(jax.random.fold_in(_rk, 7), (1,), 0, max(1, 128 // 4) + 1, jnp.int32)
        _lenS2 = 2048 - jax.random.randint(jax.random.fold_in(_rk, 8), (1,), 0, max(1, 2048 // 4) + 1, jnp.int32)
        _ctx_4096P = jax.random.normal(jax.random.fold_in(_rk, 11), (1, 16, 512), jnp.float32)
        _ctx_4096c = jax.random.dirichlet(jax.random.fold_in(_rk, 511), 0.3 * jnp.ones((16,), jnp.float32), (1, 2048))
        _ctx_4096t = jnp.einsum('bsk,bkd->bsd', _ctx_4096c, _ctx_4096P)
        _ctx_4096t = _ctx_4096t * jax.lax.rsqrt(jnp.mean(jnp.square(_ctx_4096t)) + 1e-12) * 0.953939
        ctx_4096 = -0.00010331 + 0.999899 * (_ctx_4096t + 0.3 * jax.random.normal(jax.random.fold_in(_rk, 611), (1, 2048, 512), jnp.float32))
        return (x, ctx_4096)
    x, ctx_4096 = _rec_inputs()

    def _L0_xattn_setup():
        import jax, jax.numpy as jnp
        import numpy as np
        HEADS = 32
        KV_HEADS = 8
        HEAD_DIM = 128
        EPS = 1e-06

        def rms_norm(x, w):
            var = jnp.mean(jnp.square(x.astype(jnp.float32)), axis=-1, keepdims=True)
            return (x.astype(jnp.float32) * jax.lax.rsqrt(var + EPS)).astype(x.dtype) * w
        key = jax.random.key(seed)
        ks = jax.random.split(key, 6)
        bsz, n_lat, seq, hidden = (8, 64, 512, 512)
        return {'latents': jax.random.normal(ks[0], (bsz, n_lat, hidden), jnp.float32), 'context': jax.random.normal(ks[1], (bsz, seq, hidden), jnp.float32), 'Wq': jax.random.normal(ks[2], (hidden, HEADS * HEAD_DIM), jnp.float32) * 0.02, 'Wk': jax.random.normal(ks[3], (hidden, KV_HEADS * HEAD_DIM), jnp.float32) * 0.02, 'Wv': jax.random.normal(ks[4], (hidden, KV_HEADS * HEAD_DIM), jnp.float32) * 0.02, 'Wo': jax.random.normal(ks[5], (HEADS * HEAD_DIM, hidden), jnp.float32) * 0.02, 'q_norm_w': jnp.ones((HEAD_DIM,), jnp.float32), 'k_norm_w': jnp.ones((HEAD_DIM,), jnp.float32)}
    _L0_xattn_all = _L0_xattn_setup()
    _L0_xattn_in = {k: v for k, v in _L0_xattn_all.items() if k in ('Wq', 'Wk', 'Wv', 'Wo', 'q_norm_w', 'k_norm_w')}
    del _L0_xattn_all

    def _L0_attn_setup():
        import jax, jax.numpy as jnp
        import numpy as np
        from jax import lax
        H = 64
        P = 64
        N = 128
        G = 8
        K = 4
        D_MODEL = 512
        I = H * P
        GN = G * N
        CONV_DIM = I + 2 * GN
        PROJ = I + CONV_DIM + H
        EPS = 1e-05
        GROUP_SIZE = I // G

        def _reference_tuple_inner(hidden_states, in_proj_w, conv_weight, conv_bias, dt_bias, A_log, D, norm_weight, out_proj_w):
            B, L, _ = hidden_states.shape
            proj = jnp.einsum('bld,pd->blp', hidden_states, in_proj_w)
            gate = proj[..., :I]
            hbc = proj[..., I:I + CONV_DIM]
            dt = proj[..., -H:]
            pad = jnp.pad(hbc, ((0, 0), (K - 1, 0), (0, 0)))
            conv = conv_bias
            for k in range(K):
                conv = conv + pad[:, k:k + L, :] * conv_weight[:, k]
            xBC = jax.nn.silu(conv)
            x = xBC[..., :I].reshape(B, L, H, P)
            Bm = xBC[..., I:I + GN].reshape(B, L, G, N)
            Cm = xBC[..., I + GN:].reshape(B, L, G, N)
            hpg = H // G
            B_h = jnp.repeat(Bm, hpg, axis=2)
            C_h = jnp.repeat(Cm, hpg, axis=2)
            dt_p = jax.nn.softplus(dt + dt_bias)
            A = -jnp.exp(A_log)
            dA = jnp.exp(dt_p * A)
            dtx = dt_p[..., None] * x

            def step(state, inp):
                dA_t, dtx_t, B_t, C_t = inp
                state = state * dA_t[..., None, None] + dtx_t[..., None] * B_t[:, :, None, :]
                y_t = jnp.einsum('bhpn,bhn->bhp', state, C_t)
                return (state, y_t)
            xs = (jnp.moveaxis(dA, 1, 0), jnp.moveaxis(dtx, 1, 0), jnp.moveaxis(B_h, 1, 0), jnp.moveaxis(C_h, 1, 0))
            state0 = jnp.zeros((B, H, P, N), jnp.float32)
            final_state, ys = lax.scan(step, state0, xs)
            y = jnp.moveaxis(ys, 0, 1) + x * D[None, None, :, None]
            y = y.reshape(B, L, I)
            yg = y.reshape(B, L, G, GROUP_SIZE)
            var = jnp.mean(yg * yg, axis=-1, keepdims=True)
            yn = (yg * lax.rsqrt(var + EPS)).reshape(B, L, I) * norm_weight
            yn = yn * jax.nn.silu(gate)
            out = jnp.einsum('bli,di->bld', yn, out_proj_w)
            conv_state_new = jnp.moveaxis(hbc[:, L - (K - 1):, :], 1, 2)
            return (out, conv_state_new, final_state)
        key = jax.random.key(seed)
        ks = jax.random.split(key, 6)
        B, L = (2, 256)
        s = 0.02
        return {'hidden_states': jax.random.normal(ks[0], (B, L, D_MODEL), jnp.float32), 'in_proj_w': jax.random.normal(ks[1], (PROJ, D_MODEL), jnp.float32) * s, 'conv_weight': jax.random.normal(ks[2], (CONV_DIM, K), jnp.float32) * s, 'conv_bias': jnp.zeros((CONV_DIM,), jnp.float32), 'dt_bias': jnp.ones((H,), jnp.float32), 'A_log': jnp.log(jnp.arange(1, H + 1, dtype=jnp.float32)), 'D': jnp.ones((H,), jnp.float32), 'norm_weight': jnp.ones((I,), jnp.float32), 'out_proj_w': jax.random.normal(ks[3], (D_MODEL, I), jnp.float32) * s}
    _L0_attn_all = _L0_attn_setup()
    _L0_attn_in = {k: v for k, v in _L0_attn_all.items() if k in ('in_proj_w', 'conv_weight', 'conv_bias', 'dt_bias', 'A_log', 'D', 'norm_weight', 'out_proj_w')}
    del _L0_attn_all

    def _L0_ffn_setup():
        import jax, jax.numpy as jnp
        import numpy as np
        LORA_RANK = 16
        LORA_ALPHA = 16
        LORA_SCALE = LORA_ALPHA / LORA_RANK
        key = jax.random.key(seed)
        k1, k2, k3, k4, k5 = jax.random.split(key, 5)
        B, S, D_IN, D_OUT, N_LORA, R = (8, 256, 512, 512, 3, LORA_RANK)
        std = 1.0 / np.sqrt(D_IN)
        x = jax.random.normal(k1, (B, S, D_IN), dtype=jnp.float32)
        weight = jax.random.truncated_normal(k2, -3.0, 3.0, (D_OUT, D_IN), dtype=jnp.float32) * std
        bias = jax.random.normal(k3, (D_OUT,), dtype=jnp.float32) * 0.01
        lora_A = jax.random.normal(k4, (N_LORA, R, D_IN), dtype=jnp.float32) * std
        lora_B = jax.random.normal(k5, (N_LORA, D_OUT, R), dtype=jnp.float32) * 0.02
        lora_start_indices = jnp.arange(4, dtype=jnp.int64) * 2
        return {'x': x, 'weight': weight, 'bias': bias, 'lora_A': lora_A, 'lora_B': lora_B, 'lora_start_indices': lora_start_indices}
    _L0_ffn_all = _L0_ffn_setup()
    _L0_ffn_in = {k: v for k, v in _L0_ffn_all.items() if k in ('weight', 'bias', 'lora_A', 'lora_B', 'lora_start_indices')}
    del _L0_ffn_all
    return {'x': x, 'ctx_4096': ctx_4096, 'L0_xattn_Wq': _L0_xattn_in['Wq'], 'L0_xattn_Wk': _L0_xattn_in['Wk'], 'L0_xattn_Wv': _L0_xattn_in['Wv'], 'L0_xattn_Wo': _L0_xattn_in['Wo'], 'L0_xattn_q_norm_w': _L0_xattn_in['q_norm_w'], 'L0_xattn_k_norm_w': _L0_xattn_in['k_norm_w'], 'L0_attn_in_proj_w': _L0_attn_in['in_proj_w'], 'L0_attn_conv_weight': _L0_attn_in['conv_weight'], 'L0_attn_conv_bias': _L0_attn_in['conv_bias'], 'L0_attn_dt_bias': _L0_attn_in['dt_bias'], 'L0_attn_A_log': _L0_attn_in['A_log'], 'L0_attn_D': _L0_attn_in['D'], 'L0_attn_norm_weight': _L0_attn_in['norm_weight'], 'L0_attn_out_proj_w': _L0_attn_in['out_proj_w'], 'L0_ffn_weight': _L0_ffn_in['weight'], 'L0_ffn_bias': _L0_ffn_in['bias'], 'L0_ffn_lora_A': _L0_ffn_in['lora_A'], 'L0_ffn_lora_B': _L0_ffn_in['lora_B'], 'L0_ffn_lora_start_indices': _L0_ffn_in['lora_start_indices']}

def reference(x, ctx_4096, L0_xattn_Wq, L0_xattn_Wk, L0_xattn_Wv, L0_xattn_Wo, L0_xattn_q_norm_w, L0_xattn_k_norm_w, L0_attn_in_proj_w, L0_attn_conv_weight, L0_attn_conv_bias, L0_attn_dt_bias, L0_attn_A_log, L0_attn_D, L0_attn_norm_weight, L0_attn_out_proj_w, L0_ffn_weight, L0_ffn_bias, L0_ffn_lora_A, L0_ffn_lora_B, L0_ffn_lora_start_indices):
    import jax
    import jax.numpy as jnp

    def _L0_xattn_ref(latents, context, Wq, Wk, Wv, Wo, q_norm_w, k_norm_w):
        import jax, jax.numpy as jnp
        import numpy as np
        HEADS = 32
        KV_HEADS = 8
        HEAD_DIM = 128
        EPS = 1e-06

        def rms_norm(x, w):
            var = jnp.mean(jnp.square(x.astype(jnp.float32)), axis=-1, keepdims=True)
            return (x.astype(jnp.float32) * jax.lax.rsqrt(var + EPS)).astype(x.dtype) * w
        bsz, q_len, hidden = latents.shape
        kv = jnp.concatenate([context, latents], axis=1)
        kv_len = kv.shape[1]
        groups = HEADS // KV_HEADS
        q = (latents @ Wq).reshape(bsz, q_len, HEADS, HEAD_DIM).transpose(0, 2, 1, 3)
        k = (kv @ Wk).reshape(bsz, kv_len, KV_HEADS, HEAD_DIM).transpose(0, 2, 1, 3)
        v = (kv @ Wv).reshape(bsz, kv_len, KV_HEADS, HEAD_DIM).transpose(0, 2, 1, 3)
        q = rms_norm(q, q_norm_w)
        k = rms_norm(k, k_norm_w)
        qg = q.reshape(bsz, KV_HEADS, groups, q_len, HEAD_DIM)
        scale = 1.0 / np.sqrt(HEAD_DIM)
        scores = jnp.einsum('bhgqd,bhkd->bhgqk', qg, k) * scale
        probs = jax.nn.softmax(scores.astype(jnp.float32), axis=-1).astype(q.dtype)
        out = jnp.einsum('bhgqk,bhkd->bhgqd', probs, v)
        out = out.reshape(bsz, HEADS, q_len, HEAD_DIM).transpose(0, 2, 1, 3)
        out = out.reshape(bsz, q_len, HEADS * HEAD_DIM)
        return out @ Wo

    def _L0_attn_ref(hidden_states, in_proj_w, conv_weight, conv_bias, dt_bias, A_log, D, norm_weight, out_proj_w):
        import jax, jax.numpy as jnp
        import numpy as np
        from jax import lax
        H = 64
        P = 64
        N = 128
        G = 8
        K = 4
        D_MODEL = 512
        I = H * P
        GN = G * N
        CONV_DIM = I + 2 * GN
        PROJ = I + CONV_DIM + H
        EPS = 1e-05
        GROUP_SIZE = I // G

        def _reference_tuple_inner(hidden_states, in_proj_w, conv_weight, conv_bias, dt_bias, A_log, D, norm_weight, out_proj_w):
            B, L, _ = hidden_states.shape
            proj = jnp.einsum('bld,pd->blp', hidden_states, in_proj_w)
            gate = proj[..., :I]
            hbc = proj[..., I:I + CONV_DIM]
            dt = proj[..., -H:]
            pad = jnp.pad(hbc, ((0, 0), (K - 1, 0), (0, 0)))
            conv = conv_bias
            for k in range(K):
                conv = conv + pad[:, k:k + L, :] * conv_weight[:, k]
            xBC = jax.nn.silu(conv)
            x = xBC[..., :I].reshape(B, L, H, P)
            Bm = xBC[..., I:I + GN].reshape(B, L, G, N)
            Cm = xBC[..., I + GN:].reshape(B, L, G, N)
            hpg = H // G
            B_h = jnp.repeat(Bm, hpg, axis=2)
            C_h = jnp.repeat(Cm, hpg, axis=2)
            dt_p = jax.nn.softplus(dt + dt_bias)
            A = -jnp.exp(A_log)
            dA = jnp.exp(dt_p * A)
            dtx = dt_p[..., None] * x

            def step(state, inp):
                dA_t, dtx_t, B_t, C_t = inp
                state = state * dA_t[..., None, None] + dtx_t[..., None] * B_t[:, :, None, :]
                y_t = jnp.einsum('bhpn,bhn->bhp', state, C_t)
                return (state, y_t)
            xs = (jnp.moveaxis(dA, 1, 0), jnp.moveaxis(dtx, 1, 0), jnp.moveaxis(B_h, 1, 0), jnp.moveaxis(C_h, 1, 0))
            state0 = jnp.zeros((B, H, P, N), jnp.float32)
            final_state, ys = lax.scan(step, state0, xs)
            y = jnp.moveaxis(ys, 0, 1) + x * D[None, None, :, None]
            y = y.reshape(B, L, I)
            yg = y.reshape(B, L, G, GROUP_SIZE)
            var = jnp.mean(yg * yg, axis=-1, keepdims=True)
            yn = (yg * lax.rsqrt(var + EPS)).reshape(B, L, I) * norm_weight
            yn = yn * jax.nn.silu(gate)
            out = jnp.einsum('bli,di->bld', yn, out_proj_w)
            conv_state_new = jnp.moveaxis(hbc[:, L - (K - 1):, :], 1, 2)
            return (out, conv_state_new, final_state)
        return _reference_tuple_inner(hidden_states, in_proj_w, conv_weight, conv_bias, dt_bias, A_log, D, norm_weight, out_proj_w)[0]

    def _L0_ffn_ref(x, weight, bias, lora_A, lora_B, lora_start_indices):
        import jax, jax.numpy as jnp
        import numpy as np
        LORA_RANK = 16
        LORA_ALPHA = 16
        LORA_SCALE = LORA_ALPHA / LORA_RANK
        y = jnp.einsum('bsd,od->bso', x, weight) + bias
        B = x.shape[0]
        seg = jnp.searchsorted(lora_start_indices, jnp.arange(B), side='right') - 1
        adapter_idx = jnp.clip(seg - 1, 0, lora_A.shape[0] - 1)
        A = lora_A[adapter_idx]
        Bw = lora_B[adapter_idx]
        lo = jnp.einsum('bsr,bor->bso', jnp.einsum('bsd,brd->bsr', x, A), Bw) * LORA_SCALE
        use_lora = (seg > 0)[:, None, None]
        return y + jnp.where(use_lora, lo, jnp.zeros((), dtype=y.dtype))
    x = x + _L0_xattn_ref(_layernorm(x, axis=-1), ctx_4096, L0_xattn_Wq, L0_xattn_Wk, L0_xattn_Wv, L0_xattn_Wo, L0_xattn_q_norm_w, L0_xattn_k_norm_w)
    x = x + _L0_attn_ref(_layernorm(x, axis=-1), L0_attn_in_proj_w, L0_attn_conv_weight, L0_attn_conv_bias, L0_attn_dt_bias, L0_attn_A_log, L0_attn_D, L0_attn_norm_weight, L0_attn_out_proj_w)
    x = x + _L0_ffn_ref(_layernorm(x, axis=-1), L0_ffn_weight, L0_ffn_bias, L0_ffn_lora_A, L0_ffn_lora_B, L0_ffn_lora_start_indices)
    return x

_drawn_inputs = setup_inputs


def setup_inputs(seed=0):
    import zlib

    import numpy as np

    out = dict(_drawn_inputs(seed))
    spreads = {'L0_xattn_q_norm_w': (1.0, 0.6),
     'L0_xattn_k_norm_w': (1.0, 0.6),
     'L0_attn_conv_bias': (0.0, 0.1),
     'L0_attn_dt_bias': (1.0, 0.6),
     'L0_attn_D': (1.0, 0.2),
     'L0_attn_norm_weight': (1.0, 0.2)}
    factors = {'L0_attn_A_log': 8.0, 'L0_ffn_bias': 8.0}
    for name, (base, spread) in spreads.items():
        noise = np.random.default_rng([zlib.crc32(name.encode()), seed]).standard_normal(out[name].shape)
        drawn = base * np.exp(spread * noise) if base else spread * noise
        out[name] = jnp.asarray(drawn.astype(out[name].dtype))
    for name, factor in factors.items():
        out[name] = (out[name] * factor).astype(out[name].dtype)
    return out
```

```python
from contextlib import ExitStack

import numpy as np
import concourse.bass as bass
from concourse import mybir

F32 = mybir.dt.float32
F32R = mybir.dt.float32r
I32 = mybir.dt.int32
ALU = mybir.AluOpType
ACT = mybir.ActivationFunctionType
AX = mybir.AxisListType

P = 128
Q = 128
CTX = 2048
KV = CTX + Q
DM = 512
DC = DM // P
HD = 128
HEADS, GROUPS = 32, 8
HPG = HEADS // GROUPS
TILES = KV // P
CHUNK = 512
CHUNKS = CTX // CHUNK
PARTS = CHUNKS + 1
SCORE_BANKS = 5
KT_BATCH = 4
KT_BATCHES = -(-TILES // KT_BATCH)
KN_SLOTS = 2 * KT_BATCH
RMS_EPS = 1e-6
MH, MP, MN, MG = 64, 64, 128, 8
MI = MH * MP
GW = MI // MG
GH = MH // MG
CONV = MI + 2 * MG * MN
TAPS = 4
XBC_TILES = CONV // P
X_TILES = MI // P
BLK = 512
XBC_BLKS, GATE_BLKS = CONV // BLK, MI // BLK
TPB = BLK // P
LN_EPS = 1e-5
ADAPTERS, RANK = 3, 16
AR = ADAPTERS * RANK


def perceiver_program(nc, x, ctx_t, wq, wkv, wo, q_norm, k_norm, w_xbc, w_gate, w_dt, conv_w, conv_b,
                      dt_bias, a_log, d_skip, norm_w, w_out, ffn_w, ffn_b, lora_a, lora_b, starts, picks, out):
    st = ExitStack()
    with st:
        def sem(name):
            return st.enter_context(nc.semaphore(name))

        def sb(name, shape, dt=F32):
            return st.enter_context(nc.sbuf_tensor(name, shape, dt))

        ident = sb("ident", [P, P])
        res = sb("res", [P, DM])
        xn = sb("xn", [P, DM])
        stats = sb("stats", [P, 6])
        mv = sb("mv", [P, 2])
        rstd = sb("rstd", [P, 1])
        neghalf = sb("neghalf", [P, 64])
        zero1 = sb("zero1", [P, 1])
        qkw = sb("qkw", [P, 4])
        bank = [st.enter_context(nc.psum_tensor(f"bank{n}", [P, 512], F32)) for n in range(8)]

        at = ExitStack()

        def asb(name, shape, dt=F32):
            return at.enter_context(nc.sbuf_tensor(name, shape, dt))

        kv_hi = asb("kv_hi", [P, DC, KV], F32R)
        kv_lo = asb("kv_lo", [P, DC, KV], F32R)
        kt_hi = asb("kt_hi", [P, KV], F32R)
        kt_lo = asb("kt_lo", [P, KV], F32R)
        v_hi = asb("v_hi", [P, TILES, HD], F32R)
        v_lo = asb("v_lo", [P, TILES, HD], F32R)
        probs = asb("probs", [P, HPG, KV])
        wkv_raw = asb("wkv_raw", [P, DC, 2 * HD])
        wkv_hi = asb("wkv_hi", [P, DC, 2 * HD], F32R)
        wkv_lo = asb("wkv_lo", [P, DC, 2 * HD], F32R)
        wx_raw = asb("wx_raw", [P, 4, DM])
        wx_hi = asb("wx_hi", [P, 4, DM], F32R)
        wx_lo = asb("wx_lo", [P, 4, DM], F32R)
        qt_hi = asb("qt_hi", [P, HPG * Q], F32R)
        qt_lo = asb("qt_lo", [P, HPG * Q], F32R)
        q_raw = asb("q_raw", [P, HPG, HD])
        q_tmp = asb("q_tmp", [P, HPG, HD])
        pt_hi = [asb(f"pt_hi{n}", [P, HPG * Q], F32R) for n in range(2)]
        pt_lo = [asb(f"pt_lo{n}", [P, HPG * Q], F32R) for n in range(2)]
        o_hi = asb("o_hi", [P, HPG * Q], F32R)
        o_lo = asb("o_lo", [P, HPG * Q], F32R)
        kn = asb("kn", [P, KN_SLOTS, HD])
        junk = asb("junk", [P, HD])
        k_ms = asb("k_ms", [P, TILES])
        k_rs = asb("k_rs", [P, TILES])
        q_ms = asb("q_ms", [P, HPG])
        q_rs = asb("q_rs", [P, HPG])
        rms_eps = asb("rms_eps", [P, HPG])
        inv_hd = asb("inv_hd", [P, HPG])
        part_max = asb("part_max", [P, HPG, PARTS])
        neg_max = asb("neg_max", [P, HPG])
        part_sum = asb("part_sum", [P, HPG, PARTS])
        row_sum = asb("row_sum", [P, HPG])
        inv_sum = asb("inv_sum", [P, HPG])
        at.close()

        w_in = [sb(f"w_in{n}", [P, DC, BLK]) for n in range(8)]
        xnt = sb("xnt", [P, DC, Q])
        wdt = sb("wdt", [P, DC, MH])
        cw = sb("cw", [P, XBC_TILES, TAPS])
        cb = sb("cb", [P, XBC_TILES])
        dtb = sb("dtb", [P, MH])
        alog = sb("alog", [P, MH])
        dskip = sb("dskip", [P, MH])
        sp_t = sb("sp_t", [P, 6, MH])
        neg_a = sb("neg_a", [P, MH])
        dt = sb("dt", [P, MH])
        a_dt = sb("a_dt", [P, MH])
        after = sb("after", [P, P])
        upto = sb("upto", [P, P])
        g_ms = sb("g_ms", [P, MG])
        g_rs = sb("g_rs", [P, MG])
        bc_t = sb("bc_t", [P, 2 * MG, Q])
        xc_t = [sb(f"xc_t{n}", [P, TPB, Q]) for n in range(2)]
        cacc = [sb(f"cacc{n}", [P, TPB, Q]) for n in range(2)]
        xs = sb("xs", [P, MI])
        gate = sb("gate", [P, MI])
        sg = [sb(f"sg{n}", [P, BLK]) for n in range(2)]
        gm = [sb(f"gm{n}", [P, P]) for n in range(2)]
        seg = [sb(f"seg{n}", [P, GH, P]) for n in range(2)]
        dec = [sb(f"dec{n}", [P, GH, P]) for n in range(2)]
        y = [sb(f"y{n}", [P, GW]) for n in range(2)]
        yt = [sb(f"yt{n}", [P, TPB, Q]) for n in range(2)]
        dtx = [sb(f"dtx{n}", [P, GW]) for n in range(2)]
        xd = [sb(f"xd{n}", [P, GW]) for n in range(2)]
        lw = sb("lw", [P, DC, DM])
        la = sb("la", [P, DC, AR])
        lb = sb("lb", [AR, DM])
        lbias = sb("lbias", [P, DM])
        lst = sb("lst", [AR, 4], I32)
        lstf = sb("lstf", [AR, 4])
        lcnt = sb("lcnt", [AR, 1])
        lrow = sb("lrow", [AR, 1])
        lmask = sb("lmask", [AR, 4])
        lt = sb("lt", [AR, Q])
        fin = sb("fin", [P, DM])

        x_in = sem("x_in")
        small_in = sem("small_in")
        ctx_in = [sem(f"ctx_in{n}") for n in range(CHUNKS)]
        wkv_in = sem("wkv_in")
        wx_in = sem("wx_in")
        const_ok = sem("const_ok")
        ctx_hi_ok = sem("ctx_hi_ok")
        ctx_lo_ok = sem("ctx_lo_ok")
        ln_var = sem("ln_var")
        ln_rs = sem("ln_rs")
        ln_out = sem("ln_out")
        ln_tp = sem("ln_tp")
        xt_hi_ok = sem("xt_hi_ok")
        xt_lo_ok = sem("xt_lo_ok")
        wkv_hi_ok = sem("wkv_hi_ok")
        wkv_ok = sem("wkv_ok")
        wx_hi_ok = sem("wx_hi_ok")
        wx_ok = sem("wx_ok")
        last_scores = sem("last_scores")
        scores = sem("scores")
        part_max_ok = sem("part_max_ok")
        max_ok = sem("max_ok")
        exp_ok = sem("exp_ok")
        sum_ok = sem("sum_ok")
        inv_ok = sem("inv_ok")
        q_done = sem("q_done")
        q_raw_ok = sem("q_raw_ok")
        q_sq_ok = sem("q_sq_ok")
        q_ms_ok = sem("q_ms_ok")
        q_rs_ok = sem("q_rs_ok")
        qn_ok = sem("qn_ok")
        q_tp = sem("q_tp")
        qt_ok = sem("qt_ok")
        qt_hi_ok = sem("qt_hi_ok")
        qt_lo_ok = sem("qt_lo_ok")
        kv_done = sem("kv_done")
        k_ms_ok = sem("k_ms_ok")
        k_rs_ok = sem("k_rs_ok")
        kn_ok = sem("kn_ok")
        v_hi_ok = sem("v_hi_ok")
        v_lo_ok = sem("v_lo_ok")
        k_tp = sem("k_tp")
        kt_hi_ok = sem("kt_hi_ok")
        kt_lo_ok = sem("kt_lo_ok")
        p_tp = sem("p_tp")
        pt_hi_ok = sem("pt_hi_ok")
        pt_lo_ok = sem("pt_lo_ok")
        pv_done = sem("pv_done")
        o_hi_ok = sem("o_hi_ok")
        o_lo_ok = sem("o_lo_ok")
        wo_done = sem("wo_done")
        res_ok = sem("res_ok")
        dve_step = sem("dve_step")
        pool_step = sem("pool_step")
        act_step = sem("act_step")

        w_in_in = [sem(f"w_in_in{n}") for n in range(8)]
        small2_in = sem("small2_in")
        w_out_in = [sem(f"w_out_in{n}") for n in range(8)]
        ffn_in = sem("ffn_in")
        xnt_ok = sem("xnt_ok")
        dt_done = sem("dt_done")
        blk_done = sem("blk_done")
        tap0_ok = sem("tap0_ok")
        taps_ok = sem("taps_ok")
        conv_ok = sem("conv_ok")
        x_tp = sem("x_tp")
        xs_ok = sem("xs_ok")
        gate_ok = sem("gate_ok")
        gatew_ok = sem("gatew_ok")
        sp_act = sem("sp_act")
        sp_dve = sem("sp_dve")
        dt_ok = sem("dt_ok")
        cb_done = sem("cb_done")
        gm_ok = sem("gm_ok")
        seg_ok = sem("seg_ok")
        seg_done = sem("seg_done")
        dec_ok = sem("dec_ok")
        mix_ok = sem("mix_ok")
        dtx_ok = sem("dtx_ok")
        xd_ok = sem("xd_ok")
        y_done = sem("y_done")
        y_ok = sem("y_ok")
        g_ms_ok = sem("g_ms_ok")
        g_rs_ok = sem("g_rs_ok")
        yn_ok = sem("yn_ok")
        y_tp = sem("y_tp")
        yt_ok = sem("yt_ok")
        op_done = sem("op_done")
        la_done = sem("la_done")
        lt_ok = sem("lt_ok")
        ffn_done = sem("ffn_done")
        fin_ok = sem("fin_ok")
        out_done = sem("out_done")

        LOOPED = GROUPS - 1
        SMALL2, FFN_LOADS = 7, 6
        N_BLKS = XBC_BLKS + GATE_BLKS
        W_OUT_AT = N_BLKS % 8
        N_SC = HPG * CHUNKS
        N_EX = HPG * PARTS
        PIECE = 512
        block = st.enter_context(nc.Block())

        def kv_bank(j):
            return bank[2 + j % 3]

        def batch_tiles(b):
            return range(KT_BATCH * b, min(KT_BATCH * b + KT_BATCH, TILES))

        @block.sync
        def _(sp):
            sp.dma_start(res[:, :], x).then_inc(x_in, 16)
            sp.dma_start(qkw[:, 0:1], q_norm).then_inc(small_in, 16)
            sp.dma_start(qkw[:, 1:2], k_norm).then_inc(small_in, 16)
            sp.dma_start(wkv_raw[:, :, :], wkv[0]).then_inc(wkv_in, 16)
            for n in range(CHUNKS):
                sp.dma_start(probs[:, :, n * CHUNK:(n + 1) * CHUNK], ctx_t[:, :, n * CHUNK:(n + 1) * CHUNK])\
                    .then_inc(ctx_in[n], 16)
                if n == 0:
                    sp.dma_start(wx_raw[:, :, :], wq[0]).then_inc(wx_in, 16)

            def load_next_projections(i):
                sp.wait_ge(wkv_ok, i + 1)
                sp.dma_start(wkv_raw[:, :, :], wkv[bass.ds(i + 1, 1)].rearrange("g p c n -> p (g c) n")).then_inc(wkv_in, 16)
                sp.wait_ge(wx_ok, i * 2 + 1)
                sp.dma_start(wx_raw[:, :, :], wq[bass.ds(i + 1, 1)].rearrange("g p c n -> p (g c) n")).then_inc(wx_in, 16)
                sp.wait_ge(wx_ok, i * 2 + 2)
                sp.dma_start(wx_raw[:, :, :], wo[bass.ds(i, 1)].rearrange("g p c n -> p (g c) n")).then_inc(wx_in, 16)

            with sp.Fori(0, LOOPED) as i:
                load_next_projections(i)
            sp.wait_ge(wx_ok, 2 * LOOPED + 1)
            sp.dma_start(wx_raw[:, :, :], wo[LOOPED]).then_inc(wx_in, 16)

            sp.wait_ge(kv_done, TILES * GROUPS)
            w_blocks = [w_xbc[n] for n in range(XBC_BLKS)] + [w_gate[n] for n in range(GATE_BLKS)]
            for n in range(8):
                sp.dma_start(w_in[n][:, :, :], w_blocks[n]).then_inc(w_in_in[n], 16)
            sp.wait_ge(res_ok, HPG * GROUPS + 1)
            for dst, src in ((wdt[:, :, :], w_dt), (cw[:, :, :], conv_w), (cb[:, :], conv_b),
                             (dtb[:, :], dt_bias.broadcast_to([P, MH])), (alog[:, :], a_log.broadcast_to([P, MH])),
                             (dskip[:, :], d_skip.broadcast_to([P, MH]))):
                sp.dma_start(dst, src).then_inc(small2_in, 16)
            sp.dma_start(gate[:, :], norm_w.broadcast_to([P, MI])).then_inc(small2_in, 16)
            for dst, src in ((lw[:, :, :], ffn_w), (la[:, :, :], lora_a), (lb[:, :], lora_b),
                             (lbias[:, :], ffn_b.broadcast_to([P, DM])), (lst[:, :], starts.broadcast_to([AR, 4])),
                             (lrow[:, :], picks)):
                sp.dma_start(dst, src).then_inc(ffn_in, 16)
            for n in range(8, len(w_blocks)):
                sp.wait_ge(blk_done, n - 7)
                sp.dma_start(w_in[n % 8][:, :, :], w_blocks[n]).then_inc(w_in_in[n % 8], 16)
            for g in range(MG):
                sp.wait_ge(blk_done, N_BLKS - 8 + g + 1)
                sp.dma_start(w_in[(W_OUT_AT + g) % 8][:, :, :], w_out[g]).then_inc(w_out_in[g], 16)
            sp.wait_ge(fin_ok, 1)
            sp.dma_start(out, fin[:, :]).then_inc(out_done, 16)
            sp.wait_ge(out_done, 16)

        @block.gpsimd
        def _(pool):
            steps = [0]

            def link(ins):
                steps[0] += 1
                ins.then_inc(pool_step, 1)
                pool.wait_ge(pool_step, steps[0])

            nc.gpsimd.memset(neghalf[:, :], -0.5).then_inc(const_ok, 1)
            nc.gpsimd.memset(zero1[:, :], 0.0).then_inc(const_ok, 1)
            nc.gpsimd.memset(rms_eps[:, :], RMS_EPS).then_inc(const_ok, 1)
            nc.gpsimd.memset(inv_hd[:, :], 1.0 / HD).then_inc(const_ok, 1)
            link(nc.gpsimd.memset(ident[:, :], 0.0))
            nc.gpsimd.affine_select(out=ident[:, :], in_=ident[:, :], compare_op=ALU.not_equal, fill=1.0, base=0,
                                    pattern=[[-1, P]], channel_multiplier=1).then_inc(const_ok, 1)
            pool.wait_ge(const_ok, 5)

            def layernorm_root(n):
                pool.wait_ge(ln_var, n)
                nc.gpsimd.tensor_tensor(rstd[:, :], mv[:, 1:2], neghalf[:, 0:1], ALU.pow).then_inc(ln_rs, 1)

            def weights_lo(hi_ready, count, raw, hi, lo, done, cols):
                pool.wait_ge(hi_ready, count)
                r, h, l = (t[:, :, :].rearrange("p c n -> p (c n)") for t in (raw, hi, lo))
                for at_ in range(0, cols, PIECE):
                    s = slice(at_, at_ + PIECE)
                    last = nc.gpsimd.tensor_tensor(l[:, s], r[:, s], h[:, s], ALU.subtract)
                last.then_inc(done, 1)

            def key_root(p, j):
                pool.wait_ge(k_ms_ok, p * TILES + (j + 1))
                nc.gpsimd.tensor_tensor(k_rs[:, j:j + 1], k_ms[:, j:j + 1], rms_eps[:, 0:1], ALU.add).then_inc(k_rs_ok, 1)
                pool.wait_ge(k_rs_ok, p * (2 * TILES) + (2 * j + 1))
                nc.gpsimd.tensor_tensor(k_rs[:, j:j + 1], k_rs[:, j:j + 1], neghalf[:, 0:1], ALU.pow).then_inc(k_rs_ok, 1)

            def query_root(p):
                pool.wait_ge(q_ms_ok, p + 1)
                nc.gpsimd.tensor_tensor(q_rs[:, :], q_ms[:, :], inv_hd[:, :], ALU.mult).then_inc(q_rs_ok, 1)
                pool.wait_ge(q_rs_ok, p * 3 + 1)
                nc.gpsimd.tensor_tensor(q_rs[:, :], q_rs[:, :], rms_eps[:, :], ALU.add).then_inc(q_rs_ok, 1)
                pool.wait_ge(q_rs_ok, p * 3 + 2)
                nc.gpsimd.tensor_tensor(q_rs[:, :], q_rs[:, :], neghalf[:, 0:HPG], ALU.pow).then_inc(q_rs_ok, 1)

            layernorm_root(1)
            weights_lo(wkv_hi_ok, 1, wkv_raw, wkv_hi, wkv_lo, wkv_ok, DC * 2 * HD)
            weights_lo(wx_hi_ok, 1, wx_raw, wx_hi, wx_lo, wx_ok, 4 * DM)
            for j in range(TILES):
                key_root(0, j)
                if j == 8:
                    query_root(0)

            def group(i, more):
                if more:
                    weights_lo(wx_hi_ok, i * 2 + 2, wx_raw, wx_hi, wx_lo, wx_ok, 4 * DM)
                    weights_lo(wkv_hi_ok, i + 2, wkv_raw, wkv_hi, wkv_lo, wkv_ok, DC * 2 * HD)
                    for j in range(TILES):
                        key_root(i + 1, j)
                        if j == 3:
                            query_root(i + 1)
                        if j in (7, 9, 11, 13):
                            k = (j - 7) // 2
                            pool.wait_ge(wx_hi_ok, i * 2 + 3)
                            part = nc.gpsimd.tensor_tensor(wx_lo[:, k, :], wx_raw[:, k, :], wx_hi[:, k, :], ALU.subtract)
                            if k == 3:
                                part.then_inc(wx_ok, 1)
                else:
                    weights_lo(wx_hi_ok, i * 2 + 2, wx_raw, wx_hi, wx_lo, wx_ok, 4 * DM)

            with pool.Fori(0, LOOPED) as i:
                group(i, True)
            group(LOOPED, False)

            pool.wait_ge(res_ok, HPG * GROUPS + 1)
            link(nc.gpsimd.memset(after[:, :], 1.0))
            link(nc.gpsimd.memset(upto[:, :], 1.0))
            link(nc.gpsimd.affine_select(out=after[:, :], in_=after[:, :], compare_op=ALU.is_gt, fill=0.0, base=0,
                                         pattern=[[-1, P]], channel_multiplier=1))
            nc.gpsimd.affine_select(out=upto[:, :], in_=upto[:, :], compare_op=ALU.is_ge, fill=0.0, base=0,
                                    pattern=[[1, P]], channel_multiplier=-1).then_inc(const_ok, 1)
            layernorm_root(2)
            for g in range(MG + 1):
                if g < MG:
                    s = slice(g * GW, (g + 1) * GW)
                    x3 = xs[:, s].rearrange("p (h d) -> p h d", h=GH)
                    if g == 0:
                        pool.wait_ge(dt_ok, 2)
                        pool.wait_ge(small2_in, 16 * SMALL2)
                    pool.wait_ge(xs_ok, g + 1)
                    if g >= 2:
                        pool.wait_ge(y_done, g - 1)
                        pool.wait_ge(y_ok, g - 1)
                    nc.gpsimd.tensor_tensor(dtx[g % 2][:, :].rearrange("p (h d) -> p h d", h=GH), x3,
                                            dt[:, g * GH:(g + 1) * GH].unsqueeze(2).broadcast_to([P, GH, MP]),
                                            ALU.mult).then_inc(dtx_ok, 1)
                    nc.gpsimd.tensor_tensor(xd[g % 2][:, :].rearrange("p (h d) -> p h d", h=GH), x3,
                                            dskip[:, g * GH:(g + 1) * GH].unsqueeze(2).broadcast_to([P, GH, MP]),
                                            ALU.mult).then_inc(xd_ok, 1)
                if g >= 1:
                    r = slice(g - 1, g)
                    pool.wait_ge(g_ms_ok, g)
                    link(nc.gpsimd.tensor_scalar(g_rs[:, r], g_ms[:, r], 1.0 / GW, LN_EPS, ALU.mult, ALU.add))
                    nc.gpsimd.tensor_tensor(g_rs[:, r], g_rs[:, r], neghalf[:, 0:1], ALU.pow).then_inc(g_rs_ok, 1)
            layernorm_root(3)

        @block.scalar
        def _(act):
            def hi_part(dst, src, done):
                nc.scalar.activation(dst, src, ACT.Copy).then_inc(done, 1)

            def key_squares(p, j):
                act.wait_ge(kv_done, p * TILES + (j + 1))
                if not (isinstance(p, int) and j == 0):
                    act.wait_ge(k_ms_ok, p * TILES + j)
                nc.scalar.activation(junk[:, :], kv_bank(j)[:, 0:HD], ACT.Square, scale=HD ** -0.5,
                                     accum_out=k_ms[:, j:j + 1]).then_inc(k_ms_ok, 1)

            def values_hi(j):
                hi_part(v_hi[:, j, :], kv_bank(j)[:, HD:2 * HD], v_hi_ok)

            def keys_hi(p, b):
                t = batch_tiles(b)
                act.wait_ge(k_tp, p * KT_BATCHES + (b + 1))
                hi_part(kt_hi[:, t.start * P:t.stop * P], bank[5][:, 0:len(t) * P], kt_hi_ok)

            def queries_raw(p):
                act.wait_ge(q_done, p + 1)
                nc.scalar.activation(q_raw[:, :, :].rearrange("p h d -> p (h d)"), bank[6][:, :], ACT.Copy)\
                    .then_inc(q_raw_ok, 1)

            def queries_hi(p):
                act.wait_ge(qt_ok, p + 1)
                hi_part(qt_hi[:, :], q_tmp[:, :, :].rearrange("p h d -> p (h d)"), qt_hi_ok)

            def exps_hi(i, j):
                act.wait_ge(p_tp, i * TILES + (j + 1))
                if j >= 2:
                    act.wait_ge(pv_done, i * TILES + (j - 1))
                hi_part(pt_hi[j % 2][:, :], bank[(j + 1) % 2][:, :], pt_hi_ok)

            act.wait_ge(ctx_in[0], 16)
            hi_part(kv_hi[:, :, 0:CHUNK], probs[:, :, 0:CHUNK], ctx_hi_ok)
            act.wait_ge(ln_tp, 1)
            hi_part(kv_hi[:, :, CTX:KV], bank[0][:, :].rearrange("p (c n) -> p c n", c=DC), xt_hi_ok)
            for n in range(1, CHUNKS):
                act.wait_ge(ctx_in[n], 16)
                hi_part(kv_hi[:, :, n * CHUNK:(n + 1) * CHUNK], probs[:, :, n * CHUNK:(n + 1) * CHUNK], ctx_hi_ok)
            for j in range(TILES):
                key_squares(0, j)
                values_hi(j)
                if j == 4:
                    queries_raw(0)
                if j >= 6 and (j - 6) % KT_BATCH == 0:
                    keys_hi(0, (j - 6) // KT_BATCH)
                if j == 14:
                    queries_hi(0)
            keys_hi(0, 3)
            keys_hi(0, 4)

            def group(i, more):
                for h in range(HPG):
                    act.wait_ge(max_ok, i * HPG + (h + 1))
                    for c in range(PARTS):
                        if c < CHUNKS:
                            src, dst = bank[(CHUNKS * h + c) % SCORE_BANKS][:, :], probs[:, h, c * CHUNK:(c + 1) * CHUNK]
                        else:
                            src, dst = bank[5][:, h * P:(h + 1) * P], probs[:, h, CTX:KV]
                        nc.scalar.activation(dst, src, ACT.Exp, bias=neg_max[:, h:h + 1],
                                             accum_out=part_sum[:, h, c:c + 1]).then_inc(exp_ok, 1)
                if more:
                    queries_raw(i + 1)
                exps_hi(i, 0)
                for j in range(TILES):
                    if j + 1 < TILES:
                        exps_hi(i, j + 1)
                    if j + 1 == TILES:
                        act.wait_ge(pv_done, i * TILES + TILES)
                        hi_part(o_hi[:, :], bank[6][:, :], o_hi_ok)
                    if more:
                        key_squares(i + 1, j)
                        act.wait_ge(pv_done, i * TILES + (j + 1))
                        values_hi(j)
                        if j == 8:
                            queries_hi(i + 1)
                        if j >= 6 and (j - 6) % KT_BATCH == 0 and j < 15:
                            keys_hi(i + 1, (j - 6) // KT_BATCH)
                if more:
                    keys_hi(i + 1, 3)
                    keys_hi(i + 1, 4)

            with act.Fori(0, LOOPED) as i:
                group(i, True)
            group(LOOPED, False)

            act.wait_ge(ln_tp, 2)
            nc.scalar.activation(xnt[:, :, :].rearrange("p c n -> p (c n)"), bank[0][:, :], ACT.Copy).then_inc(xnt_ok, 1)
            act.wait_ge(small2_in, 16 * SMALL2)
            nc.scalar.activation(neg_a[:, :], alog[:, :], ACT.Exp).then_inc(sp_act, 1)
            act.wait_ge(sp_dve, 2)
            nc.scalar.activation(sp_t[:, 2, :], sp_t[:, 1, :], ACT.Exp).then_inc(sp_act, 1)
            act.wait_ge(sp_dve, 3)
            nc.scalar.activation(sp_t[:, 4, :], sp_t[:, 3, :], ACT.Ln).then_inc(sp_act, 1)

            def last_tap(n):
                act.wait_ge(blk_done, n + 1)
                if n >= 2:
                    act.wait_ge(conv_ok, n - 1)
                for t in range(TPB):
                    k = TPB * n + t
                    last = nc.scalar.activation(cacc[n % 2][:, t, :], bank[2 + n % 2][:, t * P:(t + 1) * P], ACT.Identity,
                                                scale=cw[:, k, TAPS - 1:TAPS], bias=cb[:, k:k + 1])
                last.then_inc(tap0_ok, 1)

            def conv_silu(n):
                act.wait_ge(taps_ok, n + 1)
                if n < GATE_BLKS:
                    if n >= 2:
                        act.wait_ge(x_tp, n - 1)
                    dst = xc_t[n % 2][:, :, :]
                else:
                    dst = bc_t[:, TPB * (n - GATE_BLKS):TPB * (n - GATE_BLKS + 1), :]
                nc.scalar.activation(dst, cacc[n % 2][:, :, :], ACT.Silu).then_inc(conv_ok, 1)

            def x_back(n):
                act.wait_ge(x_tp, n + 1)
                nc.scalar.activation(xs[:, n * BLK:(n + 1) * BLK], bank[4 + n % 2][:, :], ACT.Copy).then_inc(xs_ok, 1)

            for n in range(XBC_BLKS + 2):
                if n < XBC_BLKS:
                    last_tap(n)
                if 1 <= n <= XBC_BLKS:
                    conv_silu(n - 1)
                if 2 <= n < GATE_BLKS + 2:
                    x_back(n - 2)
            for n in range(GATE_BLKS):
                act.wait_ge(blk_done, XBC_BLKS + n + 1)
                if n >= 2:
                    act.wait_ge(gatew_ok, n - 1)
                nc.scalar.activation(sg[n % 2][:, :], bank[2 + n % 2][:, :], ACT.Silu).then_inc(gate_ok, 1)
            for g in range(MG + 3):
                if g < MG:
                    for half in range(2):
                        act.wait_ge(seg_done, 2 * g + half + 1)
                        if g >= 2 and half == 0:
                            act.wait_ge(y_done, g - 1)
                        nc.scalar.activation(dec[g % 2][:, 4 * half:4 * half + 4, :].rearrange("p h n -> p (h n)"),
                                             bank[half][:, :], ACT.Exp).then_inc(dec_ok, 1)
                if 1 <= g <= MG:
                    k = g - 1
                    act.wait_ge(y_ok, k + 1)
                    nc.scalar.activation(sg[0][:, :], y[k % 2][:, :], ACT.Square, accum_out=g_ms[:, k:k + 1])\
                        .then_inc(g_ms_ok, 1)
                if 2 <= g < MG + 2:
                    k = g - 2
                    act.wait_ge(y_tp, k + 1)
                    if k >= 2:
                        act.wait_ge(op_done, k - 1)
                    nc.scalar.activation(yt[k % 2][:, :, :].rearrange("p c n -> p (c n)"), bank[4 + k % 2][:, :], ACT.Copy)\
                        .then_inc(yt_ok, 1)
            act.wait_ge(ln_tp, 3)
            nc.scalar.activation(xnt[:, :, :].rearrange("p c n -> p (c n)"), bank[0][:, :], ACT.Copy).then_inc(xnt_ok, 1)

        @block.vector
        def _(dve):
            steps = [0]

            def link(ins):
                steps[0] += 1
                ins.then_inc(dve_step, 1)
                dve.wait_ge(dve_step, steps[0])

            def lo_part(dst, src, hi, done):
                nc.vector.tensor_tensor(dst, src, hi, ALU.subtract).then_inc(done, 1)

            def layernorm(n):
                link(nc.vector.bn_stats(stats[:, :], res[:, :]))
                link(nc.vector.bn_aggr(mv[:, :], stats[:, :]))
                nc.vector.tensor_scalar(mv[:, 1:2], mv[:, 1:2], LN_EPS, None, ALU.add).then_inc(ln_var, 1)
                dve.wait_ge(ln_rs, n)
                nc.vector.tensor_scalar(xn[:, :], res[:, :], mv[:, 0:1], rstd[:, 0:1], ALU.subtract, ALU.mult)\
                    .then_inc(ln_out, 1)

            def weights_hi(raw, hi, done):
                nc.vector.tensor_copy(hi[:, :, :], raw[:, :, :]).then_inc(done, 1)

            def keys_normed(p, j):
                dve.wait_ge(k_rs_ok, p * (2 * TILES) + (2 * j + 2))
                if j >= KN_SLOTS:
                    dve.wait_ge(k_tp, p * KT_BATCHES + (j // KT_BATCH - 1))
                nc.vector.tensor_scalar(kn[:, j % KN_SLOTS, :], kv_bank(j)[:, 0:HD], k_rs[:, j:j + 1], None, ALU.mult)\
                    .then_inc(kn_ok, 1)

            def values_lo(p, j):
                dve.wait_ge(v_hi_ok, p * TILES + (j + 1))
                lo_part(v_lo[:, j, :], kv_bank(j)[:, HD:2 * HD], v_hi[:, j, :], v_lo_ok)

            def keys_lo(p, b):
                t = batch_tiles(b)
                s = slice(t.start * P, t.stop * P)
                dve.wait_ge(kt_hi_ok, p * KT_BATCHES + (b + 1))
                lo_part(kt_lo[:, s], bank[5][:, 0:len(t) * P], kt_hi[:, s], kt_lo_ok)

            def queries_squares(p):
                dve.wait_ge(q_raw_ok, p + 1)
                nc.vector.tensor_tensor(q_tmp[:, :, :], q_raw[:, :, :], q_raw[:, :, :], ALU.mult).then_inc(q_sq_ok, 1)
                dve.wait_ge(q_sq_ok, p + 1)
                nc.vector.tensor_reduce(q_ms[:, :], q_tmp[:, :, :], AX.X, ALU.add).then_inc(q_ms_ok, 1)

            def queries_normed(p):
                dve.wait_ge(q_rs_ok, p * 3 + 3)
                nc.vector.tensor_tensor(q_tmp[:, :, :], q_raw[:, :, :], q_rs[:, :].unsqueeze(2).broadcast_to([P, HPG, HD]),
                                        ALU.mult).then_inc(qn_ok, 1)

            def queries_weighted(p):
                dve.wait_ge(q_tp, p + 1)
                nc.vector.tensor_scalar(q_tmp[:, :, :].rearrange("p h d -> p (h d)"), bank[7][:, :], qkw[:, 2:3], None,
                                        ALU.mult).then_inc(qt_ok, 1)

            def queries_lo(p):
                dve.wait_ge(qt_hi_ok, p + 1)
                lo_part(qt_lo[:, :], q_tmp[:, :, :].rearrange("p h d -> p (h d)"), qt_hi[:, :], qt_lo_ok)

            def exps_lo(i, j):
                dve.wait_ge(pt_hi_ok, i * TILES + (j + 1))
                lo_part(pt_lo[j % 2][:, :], bank[(j + 1) % 2][:, :], pt_hi[j % 2][:, :], pt_lo_ok)

            dve.sem_inc(res_ok, 1)
            dve.wait_ge(x_in, 16)
            dve.wait_ge(const_ok, 5)
            layernorm(1)
            dve.wait_ge(small_in, 32)
            link(nc.vector.tensor_scalar(qkw[:, 2:3], qkw[:, 0:1], qkw[:, 1:2], float(HD) ** -0.5, ALU.mult, ALU.mult))
            dve.wait_ge(wkv_in, 16)
            weights_hi(wkv_raw, wkv_hi, wkv_hi_ok)
            dve.wait_ge(xt_hi_ok, 1)
            lo_part(kv_lo[:, :, CTX:KV], bank[0][:, :].rearrange("p (c n) -> p c n", c=DC), kv_hi[:, :, CTX:KV], xt_lo_ok)
            for n in range(CHUNKS):
                s = slice(n * CHUNK, (n + 1) * CHUNK)
                dve.wait_ge(ctx_hi_ok, n + 1)
                lo_part(kv_lo[:, :, s], probs[:, :, s], kv_hi[:, :, s], ctx_lo_ok)
                if n == 0:
                    dve.wait_ge(wx_in, 16)
                    weights_hi(wx_raw, wx_hi, wx_hi_ok)
            for j in range(TILES):
                values_lo(0, j)
                if j == 5:
                    queries_squares(0)
                if j >= 1:
                    keys_normed(0, j - 1)
                if j >= 6 and (j - 6) % KT_BATCH == 0:
                    keys_lo(0, (j - 6) // KT_BATCH)
                if j == 11:
                    queries_normed(0)
                if j == 13:
                    queries_weighted(0)
                if j == 15:
                    queries_lo(0)
            keys_normed(0, TILES - 1)
            keys_lo(0, 3)
            keys_lo(0, 4)

            def group(i, more):
                if more:
                    dve.wait_ge(wx_in, i * 32 + 32)
                    dve.wait_ge(q_done, i + 1)
                    dve.wait_ge(wo_done, i * HPG + 1)
                    weights_hi(wx_raw, wx_hi, wx_hi_ok)
                    dve.wait_ge(wkv_in, i * 16 + 32)
                    dve.wait_ge(kv_done, i * TILES + TILES)
                    weights_hi(wkv_raw, wkv_hi, wkv_hi_ok)
                dve.wait_ge(last_scores, i + 1)
                nc.vector.tensor_reduce(part_max[:, :, CHUNKS], bank[5][:, :].rearrange("p (h n) -> p h n", h=HPG),
                                        AX.X, ALU.max).then_inc(part_max_ok, 1)
                for h in range(HPG):
                    for c in range(CHUNKS):
                        n = CHUNKS * h + c
                        dve.wait_ge(scores, i * N_SC + (n + 1))
                        nc.vector.tensor_reduce(part_max[:, h, c:c + 1], bank[n % SCORE_BANKS][:, :], AX.X, ALU.max)\
                            .then_inc(part_max_ok, 1)
                    dve.wait_ge(part_max_ok, i * (N_SC + 1) + (CHUNKS * (h + 1) + 1))
                    nc.vector.tensor_reduce(neg_max[:, h:h + 1], part_max[:, h, :], AX.X, ALU.max, negate=True)\
                        .then_inc(max_ok, 1)
                exps_lo(i, 0)
                for j in range(TILES):
                    if j + 1 < TILES:
                        exps_lo(i, j + 1)
                    if j == 1:
                        dve.wait_ge(exp_ok, i * N_EX + N_EX)
                        nc.vector.tensor_reduce(row_sum[:, :], part_sum[:, :, :], AX.X, ALU.add).then_inc(sum_ok, 1)
                        dve.wait_ge(sum_ok, i + 1)
                        nc.vector.reciprocal(inv_sum[:, :], row_sum[:, :]).then_inc(inv_ok, 1)
                    if more and j >= 1:
                        keys_normed(i + 1, j - 1)
                    if j + 1 == TILES:
                        dve.wait_ge(o_hi_ok, i + 1)
                        lo_part(o_lo[:, :], bank[6][:, :], o_hi[:, :], o_lo_ok)
                    if more:
                        values_lo(i + 1, j)
                        if j == 2:
                            queries_squares(i + 1)
                        if j == 4:
                            queries_normed(i + 1)
                        if j == 7:
                            queries_weighted(i + 1)
                        if j == 9:
                            queries_lo(i + 1)
                        if j >= 6 and (j - 6) % KT_BATCH == 0 and j < 15:
                            keys_lo(i + 1, (j - 6) // KT_BATCH)
                    if j == 6:
                        if more:
                            dve.wait_ge(q_done, i + 2)
                            dve.wait_ge(wx_in, i * 32 + 48)
                        else:
                            dve.wait_ge(wo_done, i * HPG + 1)
                            dve.wait_ge(wx_in, i * 32 + 32)
                        weights_hi(wx_raw, wx_hi, wx_hi_ok)
                if more:
                    keys_normed(i + 1, TILES - 1)
                    keys_lo(i + 1, 3)
                for h in range(HPG):
                    dve.wait_ge(wo_done, i * HPG + (h + 2))
                    dve.wait_ge(res_ok, i * HPG + (h + 1))
                    if h == 0:
                        dve.wait_ge(inv_ok, i + 1)
                    nc.vector.scalar_tensor_tensor(out=res[:, :], in0=bank[7 - h % 2][:, :], scalar=inv_sum[:, h:h + 1],
                                                   in1=res[:, :], op0=ALU.mult, op1=ALU.add).then_inc(res_ok, 1)
                if more:
                    keys_lo(i + 1, 4)

            with dve.Fori(0, LOOPED) as i:
                group(i, True)
            group(LOOPED, False)

            dve.wait_ge(res_ok, HPG * GROUPS + 1)
            layernorm(2)
            dve.wait_ge(small2_in, 16 * SMALL2)
            dve.wait_ge(dt_done, 1)
            X, NA, E, U, L, T = (sp_t[:, k, :] for k in range(6))
            nc.vector.tensor_tensor(X, bank[1][:, 0:MH], dtb[:, :], ALU.add).then_inc(sp_dve, 1)
            dve.wait_ge(sp_dve, 1)
            nc.vector.scalar_tensor_tensor(out=NA, in0=X, scalar=-1.0, in1=X, op0=ALU.mult, op1=ALU.min).then_inc(sp_dve, 1)
            dve.wait_ge(sp_act, 2)
            nc.vector.tensor_scalar(U, E, 1.0, None, ALU.add).then_inc(sp_dve, 1)
            dve.wait_ge(sp_dve, 3)
            link(nc.vector.tensor_scalar(T, U, -1.0, None, ALU.add))
            link(nc.vector.tensor_scalar(NA, T, 0.0, None, ALU.is_equal))
            link(nc.vector.tensor_tensor(T, T, NA, ALU.add))
            link(nc.vector.reciprocal(T, T))
            link(nc.vector.tensor_tensor(T, T, E, ALU.mult))
            dve.wait_ge(sp_act, 3)
            link(nc.vector.tensor_tensor(T, T, L, ALU.mult))
            link(nc.vector.tensor_tensor(NA, NA, E, ALU.mult))
            link(nc.vector.tensor_tensor(T, T, NA, ALU.add))
            nc.vector.scalar_tensor_tensor(out=dt[:, :], in0=X, scalar=zero1[:, 0:1], in1=T, op0=ALU.max, op1=ALU.add)\
                .then_inc(dt_ok, 1)
            dve.wait_ge(dt_ok, 1)
            nc.vector.scalar_tensor_tensor(out=a_dt[:, :], in0=dt[:, :], scalar=-1.0, in1=neg_a[:, :],
                                           op0=ALU.mult, op1=ALU.mult).then_inc(dt_ok, 1)
            for n in range(XBC_BLKS):
                dve.wait_ge(tap0_ok, n + 1)
                for back in range(1, TAPS):
                    for t in range(TPB):
                        k = TPB * n + t
                        last = nc.vector.scalar_tensor_tensor(
                            out=cacc[n % 2][:, t, back:Q], in0=bank[2 + n % 2][:, t * P:(t + 1) * P - back],
                            scalar=cw[:, k, TAPS - 1 - back:TAPS - back], in1=cacc[n % 2][:, t, back:Q],
                            op0=ALU.mult, op1=ALU.add)
                    if back + 1 < TAPS:
                        link(last)
                last.then_inc(taps_ok, 1)
            for n in range(GATE_BLKS):
                s = slice(n * BLK, (n + 1) * BLK)
                dve.wait_ge(gate_ok, n + 1)
                nc.vector.tensor_tensor(gate[:, s], gate[:, s], sg[n % 2][:, :], ALU.mult).then_inc(gatew_ok, 1)
            dve.wait_ge(const_ok, 6)
            dve.wait_ge(dt_ok, 2)

            def segments(g):
                if g >= 2:
                    dve.wait_ge(seg_done, 2 * (g - 1))
                nc.vector.tensor_tensor(seg[g % 2][:, :, :], a_dt[:, g * GH:(g + 1) * GH].unsqueeze(2).broadcast_to([P, GH, P]),
                                        after[:, :].unsqueeze(1).broadcast_to([P, GH, P]), ALU.mult).then_inc(seg_ok, 1)

            segments(0)
            for g in range(MG + 2):
                if g + 1 < MG:
                    segments(g + 1)
                if g < MG:
                    dve.wait_ge(cb_done, g + 1)
                    nc.vector.tensor_tensor(gm[g % 2][:, :], bank[6][:, 0:P], upto[:, :], ALU.mult).then_inc(gm_ok, 1)
                    dve.wait_ge(gm_ok, g + 1)
                    for half in range(2):
                        h = slice(4 * half, 4 * half + 4)
                        dve.wait_ge(dec_ok, 2 * g + half + 1)
                        nc.vector.tensor_tensor(dec[g % 2][:, h, :], dec[g % 2][:, h, :],
                                                gm[g % 2][:, :].unsqueeze(1).broadcast_to([P, 4, P]), ALU.mult)\
                            .then_inc(mix_ok, 1)
                if 1 <= g <= MG:
                    k = g - 1
                    dve.wait_ge(y_done, k + 1)
                    dve.wait_ge(xd_ok, k + 1)
                    if k >= 2:
                        dve.wait_ge(y_tp, k - 1)
                    nc.vector.tensor_tensor(y[k % 2][:, :], bank[2 + k % 2][:, :], xd[k % 2][:, :], ALU.add).then_inc(y_ok, 1)
                    dve.wait_ge(g_rs_ok, k + 1)
                    nc.vector.scalar_tensor_tensor(out=y[k % 2][:, :], in0=y[k % 2][:, :], scalar=g_rs[:, k:k + 1],
                                                   in1=gate[:, k * GW:(k + 1) * GW], op0=ALU.mult, op1=ALU.mult)\
                        .then_inc(yn_ok, 1)
            dve.wait_ge(op_done, MG)
            link(nc.vector.tensor_tensor(res[:, :], res[:, :], bank[7][:, :], ALU.add))
            layernorm(3)

            dve.wait_ge(ffn_in, 16 * FFN_LOADS)
            link(nc.vector.tensor_copy(lstf[:, :], lst[:, :]))
            link(nc.vector.tensor_scalar(lmask[:, :], lstf[:, :], 0.0, None, ALU.is_le))
            link(nc.vector.tensor_reduce(lcnt[:, :], lmask[:, :], AX.X, ALU.add))
            link(nc.vector.tensor_tensor(lmask[:, 0:1], lcnt[:, :], lrow[:, :], ALU.is_equal))
            link(nc.vector.tensor_tensor(res[:, :], res[:, :], lbias[:, :], ALU.add))
            dve.wait_ge(la_done, 1)
            nc.vector.tensor_scalar(lt[:, :], bank[1][0:AR, 0:Q], lmask[:, 0:1], None, ALU.mult).then_inc(lt_ok, 1)
            dve.wait_ge(ffn_done, 1)
            nc.vector.tensor_tensor(fin[:, :], bank[2][:, :], res[:, :], ALU.add).then_inc(fin_ok, 1)

        @block.tensor
        def _(pe):
            def split_product(dst, a_hi, a_lo, b_hi, b_lo, start, stop):
                nc.tensor.matmul(dst, a_hi, b_hi, start=start, stop=False)
                nc.tensor.matmul(dst, a_hi, b_lo, start=False, stop=False)
                return nc.tensor.matmul(dst, a_lo, b_hi, start=False, stop=stop)

            def rows_transposed(n):
                pe.wait_ge(ln_out, n)
                for c in range(DC):
                    last = nc.tensor.transpose(bank[0][:, c * P:(c + 1) * P], xn[:, c * P:(c + 1) * P], ident[:, :])
                last.then_inc(ln_tp, 1)

            def queries():
                for c in range(DC):
                    last = split_product(bank[6][:, :], kv_hi[:, c, CTX:KV], kv_lo[:, c, CTX:KV], wx_hi[:, c, :], wx_lo[:, c, :],
                                         c == 0, c == DC - 1)
                last.then_inc(q_done, 1)

            def queries_transposed(p):
                pe.wait_ge(qn_ok, p + 1)
                for h in range(HPG):
                    last = nc.tensor.transpose(bank[7][:, h * P:(h + 1) * P], q_tmp[:, h, :], ident[:, :])
                last.then_inc(q_tp, 1)

            def keys_values(p, j):
                if j >= 3:
                    pe.wait_ge(v_lo_ok, p * TILES + (j - 2))
                    pe.wait_ge(kn_ok, p * TILES + (j - 2))
                t = slice(j * P, (j + 1) * P)
                for c in range(DC):
                    last = split_product(kv_bank(j)[:, 0:2 * HD], kv_hi[:, c, t], kv_lo[:, c, t], wkv_hi[:, c, :], wkv_lo[:, c, :],
                                         c == 0, c == DC - 1)
                last.then_inc(kv_done, 1)

            def keys_transposed(p, b):
                t = batch_tiles(b)
                pe.wait_ge(kn_ok, p * TILES + t.stop)
                if b >= 1:
                    pe.wait_ge(kt_lo_ok, p * KT_BATCHES + b)
                for k, j in enumerate(t):
                    last = nc.tensor.transpose(bank[5][:, k * P:(k + 1) * P], kn[:, j % KN_SLOTS, :], ident[:, :])
                last.then_inc(k_tp, 1)

            pe.sem_inc(wo_done, 1)
            pe.wait_ge(const_ok, 5)
            rows_transposed(1)
            for j in range(TILES):
                if j == 0:
                    pe.wait_ge(wkv_ok, 1)
                if j < CTX // P and j % (CHUNK // P) == 0:
                    pe.wait_ge(ctx_lo_ok, j // (CHUNK // P) + 1)
                if j == TILES - 1:
                    pe.wait_ge(xt_lo_ok, 1)
                if j == 4:
                    pe.wait_ge(wx_ok, 1)
                    pe.wait_ge(xt_lo_ok, 1)
                    queries()
                if j == 13:
                    queries_transposed(0)
                keys_values(0, j)
                if j >= 6 and (j - 6) % KT_BATCH == 0:
                    keys_transposed(0, (j - 6) // KT_BATCH)
            keys_transposed(0, 3)
            keys_transposed(0, 4)

            def group(i, more):
                def exps_transposed(j):
                    if j == 0:
                        pe.wait_ge(exp_ok, i * N_EX + (3 * PARTS + 1))
                    elif j == 1:
                        pe.wait_ge(exp_ok, i * N_EX + N_EX)
                    if j >= 2:
                        pe.wait_ge(pt_lo_ok, i * TILES + (j - 1))
                    for h in range(HPG):
                        last = nc.tensor.transpose(bank[(j + 1) % 2][:, h * P:(h + 1) * P], probs[:, h, j * P:(j + 1) * P],
                                                   ident[:, :])
                    last.then_inc(p_tp, 1)

                pe.wait_ge(qt_lo_ok, i + 1)
                pe.wait_ge(kt_lo_ok, i * KT_BATCHES + KT_BATCHES)
                for h in range(HPG):
                    s = slice(h * P, (h + 1) * P)
                    last = split_product(bank[5][:, s], qt_hi[:, s], qt_lo[:, s], kt_hi[:, CTX:KV], kt_lo[:, CTX:KV], True, True)
                last.then_inc(last_scores, 1)
                pe.wait_ge(v_lo_ok, i * TILES + TILES)
                for h in range(HPG):
                    s = slice(h * P, (h + 1) * P)
                    for c in range(CHUNKS):
                        n = CHUNKS * h + c
                        if n >= SCORE_BANKS:
                            m = n - SCORE_BANKS
                            pe.wait_ge(exp_ok, i * N_EX + (m // CHUNKS * PARTS + m % CHUNKS + 1))
                        k = slice(c * CHUNK, (c + 1) * CHUNK)
                        split_product(bank[n % SCORE_BANKS][:, :], qt_hi[:, s], qt_lo[:, s], kt_hi[:, k], kt_lo[:, k], True, True)\
                            .then_inc(scores, 1)
                if more:
                    pe.wait_ge(res_ok, i * HPG + 1)
                    pe.wait_ge(wx_ok, i * 2 + 2)
                    queries()
                    pe.wait_ge(wkv_ok, i + 2)
                    pe.wait_ge(exp_ok, i * N_EX + (3 * PARTS + 1))
                    keys_values(i + 1, 0)
                exps_transposed(0)
                exps_transposed(1)
                for j in range(TILES):
                    if 1 <= j < TILES - 1:
                        exps_transposed(j + 1)
                    if more and j in (6, 10, 14):
                        keys_transposed(i + 1, (j - 6) // KT_BATCH)
                    if more and j == 6:
                        queries_transposed(i + 1)
                    pe.wait_ge(pt_lo_ok, i * TILES + (j + 1))
                    if j == 0 and more:
                        pe.wait_ge(q_raw_ok, i + 2)
                    if j == 0 and not more:
                        pe.wait_ge(res_ok, i * HPG + 1)
                    split_product(bank[6][:, :], v_hi[:, j, :], v_lo[:, j, :], pt_hi[j % 2][:, :], pt_lo[j % 2][:, :],
                                  j == 0, j == TILES - 1).then_inc(pv_done, 1)
                    if more and j < TILES - 2:
                        keys_values(i + 1, j + 1)
                if more:
                    keys_values(i + 1, TILES - 1)
                    keys_transposed(i + 1, 3)
                pe.wait_ge(wx_ok, i * 2 + (3 if more else 2))
                pe.wait_ge(o_lo_ok, i + 1)
                if more:
                    pe.wait_ge(qt_ok, i + 2)
                for h in range(HPG):
                    s = slice(h * P, (h + 1) * P)
                    if h >= 2:
                        pe.wait_ge(res_ok, i * HPG + h)
                    split_product(bank[7 - h % 2][:, :], o_hi[:, s], o_lo[:, s], wx_hi[:, h, :], wx_lo[:, h, :], True, True)\
                        .then_inc(wo_done, 1)
                if more:
                    keys_transposed(i + 1, 4)

            with pe.Fori(0, LOOPED) as i:
                group(i, True)
            group(LOOPED, False)

            def product(dst, lhs, rhs):
                for c in range(DC):
                    last = nc.tensor.matmul(dst, lhs(c), rhs(c), start=c == 0, stop=c == DC - 1)
                return last

            rows_transposed(2)
            pe.wait_ge(xnt_ok, 1)
            pe.wait_ge(small2_in, 16 * SMALL2)
            product(bank[1][:, 0:MH], lambda c: xnt[:, c, :], lambda c: wdt[:, c, :]).then_inc(dt_done, 1)

            def x_transposed(n):
                pe.wait_ge(conv_ok, n + 1)
                if n >= 2:
                    pe.wait_ge(xs_ok, n - 1)
                for t in range(TPB):
                    last = nc.tensor.transpose(bank[4 + n % 2][:, t * P:(t + 1) * P], xc_t[n % 2][:, t, :], ident[:, :])
                last.then_inc(x_tp, 1)

            for n in range(XBC_BLKS + GATE_BLKS):
                pe.wait_ge(w_in_in[n % 8], 16 * (n // 8 + 1))
                w = w_in[n % 8]
                if n < XBC_BLKS:
                    if n >= 2:
                        pe.wait_ge(taps_ok, n - 1)
                    for t in range(TPB):
                        s = slice(t * P, (t + 1) * P)
                        last = product(bank[2 + n % 2][:, s], lambda c: w[:, c, s], lambda c: xnt[:, c, :])
                    last.then_inc(blk_done, 1)
                else:
                    if n < XBC_BLKS + 2:
                        pe.wait_ge(taps_ok, n - 1)
                    else:
                        pe.wait_ge(gate_ok, n - 1 - XBC_BLKS)
                    product(bank[2 + n % 2][:, :], lambda c: xnt[:, c, :], lambda c: w[:, c, :]).then_inc(blk_done, 1)
                if 2 <= n < X_TILES // TPB + 2:
                    x_transposed(n - 2)
            for g in range(MG + 3):
                if g < MG:
                    if g >= 1:
                        pe.wait_ge(gm_ok, g)
                    else:
                        pe.wait_ge(conv_ok, XBC_BLKS)
                        pe.wait_ge(const_ok, 6)
                    nc.tensor.matmul(bank[6][:, 0:P], bc_t[:, g, :], bc_t[:, MG + g, :], start=True, stop=True).then_inc(cb_done, 1)
                    pe.wait_ge(seg_ok, g + 1)
                    for half in range(2):
                        if g >= 1:
                            pe.wait_ge(dec_ok, 2 * (g - 1) + half + 1)
                        for k in range(4):
                            last = nc.tensor.matmul(bank[half][:, k * P:(k + 1) * P], seg[g % 2][:, 4 * half + k, :], upto[:, :],
                                                    start=True, stop=True)
                        last.then_inc(seg_done, 1)
                if 1 <= g <= MG:
                    k = g - 1
                    pe.wait_ge(mix_ok, 2 * k + 2)
                    pe.wait_ge(dtx_ok, k + 1)
                    if k < 2:
                        pe.wait_ge(gate_ok, GATE_BLKS - 1 + k)
                    else:
                        pe.wait_ge(y_ok, k - 1)
                    for h in range(GH):
                        s = slice(h * MP, (h + 1) * MP)
                        last = nc.tensor.matmul(bank[2 + k % 2][:, s], dec[k % 2][:, h, :], dtx[k % 2][:, s], start=True, stop=True)
                    last.then_inc(y_done, 1)
                if 2 <= g < MG + 2:
                    k = g - 2
                    pe.wait_ge(yn_ok, k + 1)
                    if k >= 2:
                        pe.wait_ge(yt_ok, k - 1)
                    else:
                        pe.wait_ge(xs_ok, X_TILES // TPB)
                    for t in range(TPB):
                        s = slice(t * P, (t + 1) * P)
                        last = nc.tensor.transpose(bank[4 + k % 2][:, s], y[k % 2][:, s], ident[:, :])
                    last.then_inc(y_tp, 1)
                if g >= 3:
                    k = g - 3
                    pe.wait_ge(yt_ok, k + 1)
                    pe.wait_ge(w_out_in[k], 16)
                    for t in range(TPB):
                        last = nc.tensor.matmul(bank[7][:, :], yt[k % 2][:, t, :], w_in[(W_OUT_AT + k) % 8][:, t, :],
                                                start=k == 0 and t == 0, stop=k == MG - 1 and t == TPB - 1)
                    last.then_inc(op_done, 1)

            rows_transposed(3)
            pe.wait_ge(xnt_ok, 2)
            pe.wait_ge(ffn_in, 16 * FFN_LOADS)
            product(bank[1][0:AR, 0:Q], lambda c: la[:, c, :], lambda c: xnt[:, c, :]).then_inc(la_done, 1)
            for c in range(DC):
                nc.tensor.matmul(bank[2][:, :], xnt[:, c, :], lw[:, c, :], start=c == 0, stop=False)
            pe.wait_ge(lt_ok, 1)
            nc.tensor.matmul(bank[2][:, :], lt[:, :], lb[:, :], start=False, stop=True).then_inc(ffn_done, 1)


def kernel(**inputs):
    from concourse import bacc
    from concourse.bass_utils import run_bass_kernel_spmd

    def a(name):
        return np.asarray(inputs[name])

    def chunks(m):
        return np.ascontiguousarray(m.reshape(-1, P, m.shape[1]).transpose(1, 0, 2))

    def column_blocks(m, width):
        return np.ascontiguousarray(m.reshape(m.shape[0] // P, P, -1, width).transpose(2, 1, 0, 3))

    wk, wv = (column_blocks(a(f"L0_xattn_{n}"), HD) for n in ("Wk", "Wv"))
    w_in = a("L0_attn_in_proj_w").T
    arrays = {
        "x": a("x").reshape(Q, DM),
        "ctx_t": chunks(a("ctx_4096").reshape(CTX, DM).T),
        "wq": column_blocks(a("L0_xattn_Wq"), HPG * HD),
        "wkv": np.ascontiguousarray(np.concatenate([wk, wv], axis=3)),
        "wo": np.ascontiguousarray(a("L0_xattn_Wo").reshape(GROUPS, HPG, HD, DM).transpose(0, 2, 1, 3)),
        "q_norm": a("L0_xattn_q_norm_w").reshape(HD, 1),
        "k_norm": a("L0_xattn_k_norm_w").reshape(HD, 1),
        "w_xbc": column_blocks(w_in[:, MI:MI + CONV], BLK),
        "w_gate": column_blocks(w_in[:, :MI], BLK),
        "w_dt": chunks(w_in[:, MI + CONV:]),
        "conv_w": chunks(a("L0_attn_conv_weight")),
        "conv_b": np.ascontiguousarray(a("L0_attn_conv_bias").reshape(XBC_TILES, P).T),
        "dt_bias": a("L0_attn_dt_bias").reshape(1, MH),
        "a_log": a("L0_attn_A_log").reshape(1, MH),
        "d_skip": a("L0_attn_D").reshape(1, MH),
        "norm_w": a("L0_attn_norm_weight").reshape(1, MI),
        "w_out": np.ascontiguousarray(a("L0_attn_out_proj_w").T.reshape(MG, TPB, P, DM).transpose(0, 2, 1, 3)),
        "ffn_w": chunks(a("L0_ffn_weight").T),
        "ffn_b": a("L0_ffn_bias").reshape(1, DM),
        "lora_a": chunks(a("L0_ffn_lora_A").reshape(AR, DM).T),
        "lora_b": np.ascontiguousarray(a("L0_ffn_lora_B").transpose(0, 2, 1).reshape(AR, DM)),
        "starts": a("L0_ffn_lora_start_indices").reshape(1, 4),
        "picks": np.repeat(np.arange(ADAPTERS, dtype=np.float32) + 2, RANK).reshape(AR, 1),
    }
    nc = bacc.Bacc("TRN2", target_bir_lowering=False, num_devices=1, dynamic_dma_scratch_size=1024)
    args, given = [], {}
    for name, v in arrays.items():
        given[f"in_{name}"] = np.ascontiguousarray(v)
        args.append(nc.dram_tensor(f"in_{name}", v.shape, mybir.dt.from_np(v.dtype), kind="ExternalInput").ap())
    args.append(nc.dram_tensor("layer_out", (Q, DM), F32, kind="ExternalOutput").ap())
    perceiver_program(nc, *args)
    r = run_bass_kernel_spmd(nc, [given], core_ids=[0])
    return r.results[0]["layer_out"].reshape(1, Q, DM)
```

```python
from contextlib import ExitStack

import numpy as np
import concourse.bass as bass
from concourse import mybir

F32 = mybir.dt.float32
F32R = mybir.dt.float32r
I32 = mybir.dt.int32
ALU = mybir.AluOpType
ACT = mybir.ActivationFunctionType
AX = mybir.AxisListType

P = 128
Q = 128
CTX = 2048
KV = CTX + Q
DM = 512
DC = DM // P
HD = 128
HEADS, GROUPS = 32, 8
HPG = HEADS // GROUPS
TILES = KV // P
CHUNK = 512
CHUNKS = CTX // CHUNK
PARTS = CHUNKS + 1
SCORE_BANKS = 7
KT_BATCH = 4
KT_BATCHES = -(-TILES // KT_BATCH)
KN_SLOTS = 2 * KT_BATCH
RMS_EPS = 1e-6
MH, MP, MN, MG = 64, 64, 128, 8
MI = MH * MP
GW = MI // MG
GH = MH // MG
CONV = MI + 2 * MG * MN
TAPS = 4
XBC_TILES = CONV // P
X_TILES = MI // P
BLK = 512
BC_BLKS = 2 * MG * MN // BLK
TPB = BLK // P
LN_EPS = 1e-5
ADAPTERS, RANK = 3, 16
AR = ADAPTERS * RANK


def perceiver_program(nc, x, ctx_t, wq, wkv, wo, q_norm, k_norm, w_xbc, w_gate, w_dt, conv_w, conv_b,
                      dt_bias, a_log, d_skip, norm_w, w_out, ffn_w, ffn_b, lora_a, lora_b, starts, picks, out):
    st = ExitStack()
    with st:
        def sem(name):
            return st.enter_context(nc.semaphore(name))

        def sb(name, shape, dt=F32):
            return st.enter_context(nc.sbuf_tensor(name, shape, dt))

        ident = sb("ident", [P, P])
        res = sb("res", [P, DM])
        res_odd = sb("res_odd", [P, DM])
        xn = sb("xn", [P, DM])
        stats = sb("stats", [P, 6])
        mv = sb("mv", [P, 2])
        rstd = sb("rstd", [P, 1])
        neghalf = sb("neghalf", [P, 64])
        zero1 = sb("zero1", [P, 1])
        qkw = sb("qkw", [P, 4])
        wdt = sb("wdt", [P, DC, MH])
        cw = sb("cw", [P, XBC_TILES, TAPS])
        cb = sb("cb", [P, XBC_TILES])
        dtb = sb("dtb", [P, MH])
        alog = sb("alog", [P, MH])
        dskip = sb("dskip", [P, MH])
        bank = [st.enter_context(nc.psum_tensor(f"bank{n}", [P, 512], F32)) for n in range(8)]

        at = ExitStack()

        def asb(name, shape, dt=F32):
            return at.enter_context(nc.sbuf_tensor(name, shape, dt))

        kv_hi = asb("kv_hi", [P, DC, KV], F32R)
        kv_lo = asb("kv_lo", [P, DC, KV], F32R)
        kt_hi = asb("kt_hi", [P, KV], F32R)
        kt_lo = asb("kt_lo", [P, KV], F32R)
        v_hi = asb("v_hi", [P, TILES, HD], F32R)
        v_lo = asb("v_lo", [P, TILES, HD], F32R)
        probs = asb("probs", [P, HPG, KV])
        wkv_raw = asb("wkv_raw", [P, DC, 2 * HD])
        wkv_hi = asb("wkv_hi", [P, DC, 2 * HD], F32R)
        wkv_lo = asb("wkv_lo", [P, DC, 2 * HD], F32R)
        wx_raw = asb("wx_raw", [P, 4, DM])
        wq_hi = asb("wq_hi", [P, 4, DM], F32R)
        wq_lo = asb("wq_lo", [P, 4, DM], F32R)
        wo_hi = asb("wo_hi", [P, 4, DM], F32R)
        wo_lo = asb("wo_lo", [P, 4, DM], F32R)
        qt_hi = asb("qt_hi", [P, HPG * Q], F32R)
        qt_lo = asb("qt_lo", [P, HPG * Q], F32R)
        q_raw = asb("q_raw", [P, HPG, HD])
        q_tmp = asb("q_tmp", [P, HPG, HD])
        pt_hi = [asb(f"pt_hi{n}", [P, HPG * Q], F32R) for n in range(2)]
        pt_lo = [asb(f"pt_lo{n}", [P, HPG * Q], F32R) for n in range(2)]
        o_hi = asb("o_hi", [P, HPG * Q], F32R)
        o_lo = asb("o_lo", [P, HPG * Q], F32R)
        kn = asb("kn", [P, KN_SLOTS, HD])
        junk = asb("junk", [P, HD])
        k_ms = asb("k_ms", [P, TILES])
        k_rs = asb("k_rs", [P, TILES])
        q_ms = asb("q_ms", [P, HPG])
        q_rs = asb("q_rs", [P, HPG])
        rms_eps = asb("rms_eps", [P, HPG])
        inv_hd = asb("inv_hd", [P, HPG])
        part_max = asb("part_max", [P, HPG, PARTS])
        neg_max = asb("neg_max", [P, HPG])
        part_sum = asb("part_sum", [P, HPG, PARTS])
        row_sum = asb("row_sum", [P, HPG])
        inv_sum = asb("inv_sum", [P, HPG])
        at.close()

        w_in = [sb(f"w_in{n}", [P, DC, BLK]) for n in range(8)]
        xnt = sb("xnt", [P, DC, Q])
        xnt_hi = sb("xnt_hi", [P, DC, Q], F32R)
        xnt_lo = sb("xnt_lo", [P, DC, Q], F32R)
        wg_hi = [sb(f"wg_hi{n}", [P, DC, BLK], F32R) for n in range(2)]
        wg_lo = [sb(f"wg_lo{n}", [P, DC, BLK], F32R) for n in range(2)]
        sp_t = sb("sp_t", [P, 6, MH])
        neg_a = sb("neg_a", [P, MH])
        dt = sb("dt", [P, MH])
        a_dt = sb("a_dt", [P, MH])
        a_hi = sb("a_hi", [P, MH], F32R)
        a_lo = sb("a_lo", [P, MH], F32R)
        after = sb("after", [P, P], F32R)
        upto = sb("upto", [P, P])
        g_ms = sb("g_ms", [P, MG])
        g_rs = sb("g_rs", [P, MG])
        bc_t = sb("bc_t", [P, 2 * MG, Q])
        xc_t = [sb(f"xc_t{n}", [P, TPB, Q]) for n in range(2)]
        cacc = [sb(f"cacc{n}", [P, TPB, Q]) for n in range(2)]
        xs = sb("xs", [P, MI])
        gate = sb("gate", [P, MI])
        sg = [sb(f"sg{n}", [P, BLK]) for n in range(2)]
        sq = sb("sq", [P, GW])
        gm = sb("gm", [P, MG, P])
        seg_hi = [sb(f"seg_hi{n}", [P, GH, P], F32R) for n in range(2)]
        seg_lo = [sb(f"seg_lo{n}", [P, GH, P], F32R) for n in range(2)]
        dec = [sb(f"dec{n}", [P, GH, P]) for n in range(2)]
        y = [sb(f"y{n}", [P, GW]) for n in range(2)]
        yt = [sb(f"yt{n}", [P, TPB, Q]) for n in range(2)]
        dtx = [sb(f"dtx{n}", [P, GW]) for n in range(2)]
        xd = [sb(f"xd{n}", [P, GW]) for n in range(2)]
        la = sb("la", [P, DC, AR])
        lb = sb("lb", [AR, DM])
        lbias = sb("lbias", [P, DM])
        lst = sb("lst", [AR, 4], I32)
        lstf = sb("lstf", [AR, 4])
        lcnt = sb("lcnt", [AR, 1])
        lrow = sb("lrow", [AR, 1])
        lmask = sb("lmask", [AR, 4])
        lt = sb("lt", [AR, Q])
        fin = sb("fin", [P, DM])

        x_in = sem("x_in")
        small_in = sem("small_in")
        ctx_in = [sem(f"ctx_in{n}") for n in range(2 * CHUNKS)]
        wkv_in = sem("wkv_in")
        wx_in = sem("wx_in")
        const_ok = sem("const_ok")
        ctx_hi_ok = sem("ctx_hi_ok")
        ctx_lo_ok = sem("ctx_lo_ok")
        ln_var = sem("ln_var")
        ln_rs = sem("ln_rs")
        ln_out = sem("ln_out")
        ln_tp = sem("ln_tp")
        xt_hi_ok = sem("xt_hi_ok")
        xt_lo_ok = sem("xt_lo_ok")
        wkv_hi_ok = sem("wkv_hi_ok")
        wkv_ok = sem("wkv_ok")
        wq_hi_ok = sem("wq_hi_ok")
        wq_ok = sem("wq_ok")
        wo_hi_ok = sem("wo_hi_ok")
        wo_ok = sem("wo_ok")
        last_scores = sem("last_scores")
        scores = sem("scores")
        part_max_ok = sem("part_max_ok")
        max_ok = sem("max_ok")
        exp_ok = sem("exp_ok")
        sum_ok = sem("sum_ok")
        inv_ok = sem("inv_ok")
        q_done = sem("q_done")
        q_raw_ok = sem("q_raw_ok")
        q_sq_ok = sem("q_sq_ok")
        q_ms_ok = sem("q_ms_ok")
        q_rs_ok = sem("q_rs_ok")
        qn_ok = sem("qn_ok")
        q_tp = sem("q_tp")
        qt_ok = sem("qt_ok")
        qt_hi_ok = sem("qt_hi_ok")
        qt_lo_ok = sem("qt_lo_ok")
        kv_done = sem("kv_done")
        k_ms_ok = sem("k_ms_ok")
        k_rs_ok = sem("k_rs_ok")
        kn_ok = sem("kn_ok")
        v_hi_ok = sem("v_hi_ok")
        v_lo_ok = sem("v_lo_ok")
        k_tp = sem("k_tp")
        kt_hi_ok = sem("kt_hi_ok")
        kt_lo_ok = sem("kt_lo_ok")
        p_tp = sem("p_tp")
        pt_hi_ok = sem("pt_hi_ok")
        pt_lo_ok = sem("pt_lo_ok")
        pv_done = sem("pv_done")
        o_hi_ok = sem("o_hi_ok")
        o_lo_ok = sem("o_lo_ok")
        wo_done = sem("wo_done")
        res_ok = sem("res_ok")
        dve_step = sem("dve_step")
        pool_step = sem("pool_step")

        w_in_in = [sem(f"w_in_in{n}") for n in range(8)]
        small2_in = sem("small2_in")
        norm_in = sem("norm_in")
        ffn_in = sem("ffn_in")
        xnt_ok = sem("xnt_ok")
        xnt_hi_ok = sem("xnt_hi_ok")
        xnt_lo_ok = sem("xnt_lo_ok")
        wg_hi_ok = sem("wg_hi_ok")
        wg_lo_ok = sem("wg_lo_ok")
        dt_done = sem("dt_done")
        blk_done = sem("blk_done")
        tap0_ok = sem("tap0_ok")
        taps_ok = sem("taps_ok")
        conv_ok = sem("conv_ok")
        x_tp = sem("x_tp")
        xs_ok = sem("xs_ok")
        gate_ok = sem("gate_ok")
        gatew_ok = sem("gatew_ok")
        sp_act = sem("sp_act")
        sp_dve = sem("sp_dve")
        dt_ok = sem("dt_ok")
        cb_done = sem("cb_done")
        gm_ok = sem("gm_ok")
        seg_ok = sem("seg_ok")
        seg_lo_ok = sem("seg_lo_ok")
        a_split = sem("a_split")
        seg_done = sem("seg_done")
        dec_ok = sem("dec_ok")
        mix_ok = sem("mix_ok")
        dtx_ok = sem("dtx_ok")
        xd_ok = sem("xd_ok")
        y_done = sem("y_done")
        y_ok = sem("y_ok")
        g_ms_ok = sem("g_ms_ok")
        g_rs_ok = sem("g_rs_ok")
        yn_ok = sem("yn_ok")
        y_tp = sem("y_tp")
        yt_ok = sem("yt_ok")
        op_done = sem("op_done")
        res_final = sem("res_final")
        la_done = sem("la_done")
        lt_ok = sem("lt_ok")
        ffn_done = sem("ffn_done")
        fin_ok = sem("fin_ok")
        out_done = sem("out_done")

        LOOPED = GROUPS - 2
        SMALL_LOADS, FFN_LOADS = 6, 5
        BIG = [("bc", n) for n in range(BC_BLKS)]
        for t in range(MG + 3):
            BIG += [("x", t), ("gate", t)] if t < MG else []
            BIG += [("out", t - 3)] if t >= 3 else []
        BIG += [("linear", 0)]
        N_SC = HPG * CHUNKS
        N_EX = HPG * PARTS
        HALF = CHUNK // 2
        HALVES = CTX // HALF
        block = st.enter_context(nc.Block())

        q_bank, out_bank, key_bank = bank[2], bank[6], bank[7]

        def exp_bank(more, j):
            return bank[j % 2] if more else bank[2 + j % 4]

        def pt(more, j):
            if more or j % 4 < 2:
                return pt_hi[j % 2][:, :], pt_lo[j % 2][:, :]
            return wq_hi[:, j % 2, :], wq_lo[:, j % 2, :]

        FIRST_KV_BANKS = (4, 5, 6, 1, 3)

        def kv_bank(p, j):
            return bank[FIRST_KV_BANKS[j % 5]] if isinstance(p, int) and p == 0 else bank[3 + j % 3]

        def wo_bank(h):
            return bank[5 + h % 2]

        SCORE_ORDER = [1, 2, 0] + list(range(3, HPG * CHUNKS))
        EARLY = 5

        def exps_before(n):
            return n // CHUNKS * PARTS + n % CHUNKS + 1

        def big_buffer(kind, k):
            return w_in[BIG.index((kind, k)) % 8]

        def conv_tile(c, t):
            return X_TILES + TPB * c + t if c < BC_BLKS else TPB * (c - BC_BLKS) + t

        def conv_bank(c):
            return bank[(2, 3, 6, 0, 2, 7)[c]] if c < BC_BLKS + 2 else bank[2]

        def blocks_to(kind, k):
            at = BIG.index((kind, k))
            return sum(name in ("bc", "x", "gate") for name, _ in BIG[:at + 1])

        def batch_tiles(b):
            return range(KT_BATCH * b, min(KT_BATCH * b + KT_BATCH, TILES))

        CLOCK_FILL = (14, 14, 10)
        FIRST_WQ_STEPS = (3, 5, 7, 8)

        @block.sync
        def _(sp):
            sp.dma_start(wkv_raw[:, :, :], wkv[0]).then_inc(wkv_in, 16)
            for n in range(HALVES):
                sp.dma_start(probs[:, :, n * HALF:(n + 1) * HALF], ctx_t[:, :, n * HALF:(n + 1) * HALF])\
                    .then_inc(ctx_in[n], 16)
                if n == 1:
                    sp.dma_start(res[:, :], x).then_inc(x_in, 16)
                if n == 3:
                    sp.dma_start(wx_raw[:, :, :], wq[0]).then_inc(wx_in, 16)
                    sp.dma_start(qkw[:, 0:1], q_norm).then_inc(small_in, 16)
                    sp.dma_start(qkw[:, 1:2], k_norm).then_inc(small_in, 16)
            for dst, src in ((wdt[:, :, :], w_dt), (cw[:, :, :], conv_w), (cb[:, :], conv_b),
                             (dtb[:, :], dt_bias.broadcast_to([P, MH])), (alog[:, :], a_log.broadcast_to([P, MH])),
                             (dskip[:, :], d_skip.broadcast_to([P, MH]))):
                sp.dma_start(dst, src).then_inc(small2_in, 16)
            sp.wait_ge(wq_ok, 1)
            sp.dma_start(wx_raw[:, :, :], wq[1]).then_inc(wx_in, 16)

            def load(dst, src, g, done):
                src = src[g] if isinstance(g, int) else src[bass.ds(g, 1)].rearrange("g p c n -> p (g c) n")
                sp.dma_start(dst[:, :, :], src).then_inc(done, 16)

            def group(i, more, more_q):
                if more:
                    sp.wait_ge(wkv_ok, i + 1)
                    load(wkv_raw, wkv, i + 1, wkv_in)
                    sp.wait_ge(wq_ok, i + 2)
                else:
                    sp.wait_ge(wo_ok, i)
                load(wx_raw, wo, i, wx_in)
                if more_q:
                    sp.wait_ge(wo_ok, i + 1)
                    load(wx_raw, wq, i + 2, wx_in)

            with sp.Fori(0, LOOPED) as i:
                group(i, True, True)
            group(LOOPED, True, False)
            group(LOOPED + 1, False, False)

            sp.wait_ge(kv_done, TILES * GROUPS)
            sources = {"bc": lambda k: w_xbc[MG + k], "x": lambda k: w_xbc[k], "gate": lambda k: w_gate[k],
                       "out": lambda k: w_out[k], "linear": lambda k: ffn_w}

            def load_big(m):
                kind, k = BIG[m]
                if m >= 8:
                    kind_before, k_before = BIG[m - 8]
                    if kind_before == "out":
                        sp.wait_ge(op_done, k_before + 1)
                    elif kind_before == "gate":
                        sp.wait_ge(wg_lo_ok, DC * (k_before + 1))
                    else:
                        sp.wait_ge(blk_done, blocks_to(kind_before, k_before))
                sp.dma_start(w_in[m % 8][:, :, :], sources[kind](k)).then_inc(w_in_in[m % 8], 16)

            for m in range(8):
                load_big(m)
            sp.wait_ge(res_ok, HPG * GROUPS + 1)
            sp.dma_start(gate[:, :], norm_w.broadcast_to([P, MI])).then_inc(norm_in, 16)
            for dst, src in ((la[:, :, :], lora_a), (lb[:, :], lora_b),
                             (lbias[:, :], ffn_b.broadcast_to([P, DM])), (lst[:, :], starts.broadcast_to([AR, 4])),
                             (lrow[:, :], picks)):
                sp.dma_start(dst, src).then_inc(ffn_in, 16)
            for m in range(8, len(BIG)):
                load_big(m)
            sp.wait_ge(fin_ok, 1)
            sp.dma_start(out, fin[:, :]).then_inc(out_done, 16)
            sp.wait_ge(out_done, 16)

        @block.gpsimd
        def _(pool):
            steps = [0]

            def link(ins):
                steps[0] += 1
                ins.then_inc(pool_step, 1)
                pool.wait_ge(pool_step, steps[0])

            nc.gpsimd.memset(neghalf[:, :], -0.5).then_inc(const_ok, 1)
            nc.gpsimd.memset(zero1[:, :], 0.0).then_inc(const_ok, 1)
            nc.gpsimd.memset(rms_eps[:, :], RMS_EPS).then_inc(const_ok, 1)
            nc.gpsimd.memset(inv_hd[:, :], 1.0 / HD).then_inc(const_ok, 1)
            link(nc.gpsimd.memset(ident[:, :], 0.0))
            nc.gpsimd.affine_select(out=ident[:, :], in_=ident[:, :], compare_op=ALU.not_equal, fill=1.0, base=0,
                                    pattern=[[-1, P]], channel_multiplier=1).then_inc(const_ok, 1)
            pool.wait_ge(const_ok, 5)

            def layernorm_root(n):
                pool.wait_ge(ln_var, n)
                nc.gpsimd.tensor_tensor(rstd[:, :], mv[:, 1:2], neghalf[:, 0:1], ALU.pow).then_inc(ln_rs, 1)

            def flat(t):
                return t[:, :, :].rearrange("p c n -> p (c n)")

            def split_wkv(p):
                pool.wait_ge(wkv_in, p * 16 + 16)
                pool.wait_ge(kv_done, p * TILES)
                r, h, l = flat(wkv_raw), flat(wkv_hi), flat(wkv_lo)
                nc.gpsimd.tensor_tensor(h, r, zero1[:, 0:1].broadcast_to([P, DC * 2 * HD]), ALU.add).then_inc(wkv_hi_ok, 1)
                pool.wait_ge(wkv_hi_ok, p + 1)
                nc.gpsimd.tensor_tensor(l, r, h, ALU.subtract).then_inc(wkv_ok, 1)

            def lo_quarter(hi_ok, count, k, hi, lo, done):
                pool.wait_ge(hi_ok, count + (k + 1))
                part = nc.gpsimd.tensor_tensor(lo[:, k, :], wx_raw[:, k, :], hi[:, k, :], ALU.subtract)
                if k == 3:
                    part.then_inc(done, 1)

            def key_root(p, j):
                pool.wait_ge(k_ms_ok, p * TILES + (j + 1))
                nc.gpsimd.tensor_tensor(k_rs[:, j:j + 1], k_ms[:, j:j + 1], rms_eps[:, 0:1], ALU.add).then_inc(k_rs_ok, 1)
                pool.wait_ge(k_rs_ok, p * (2 * TILES) + (2 * j + 1))
                nc.gpsimd.tensor_tensor(k_rs[:, j:j + 1], k_rs[:, j:j + 1], neghalf[:, 0:1], ALU.pow).then_inc(k_rs_ok, 1)

            def query_root(p):
                pool.wait_ge(q_ms_ok, p + 1)
                nc.gpsimd.tensor_tensor(q_rs[:, :], q_ms[:, :], inv_hd[:, :], ALU.mult).then_inc(q_rs_ok, 1)
                pool.wait_ge(q_rs_ok, p * 3 + 1)
                nc.gpsimd.tensor_tensor(q_rs[:, :], q_rs[:, :], rms_eps[:, :], ALU.add).then_inc(q_rs_ok, 1)
                pool.wait_ge(q_rs_ok, p * 3 + 2)
                nc.gpsimd.tensor_tensor(q_rs[:, :], q_rs[:, :], neghalf[:, 0:HPG], ALU.pow).then_inc(q_rs_ok, 1)

            layernorm_root(1)
            for j in range(TILES):
                key_root(0, j)
                if j in FIRST_WQ_STEPS:
                    lo_quarter(wq_hi_ok, 0, FIRST_WQ_STEPS.index(j), wq_hi, wq_lo, wq_ok)
                if j == 12:
                    query_root(0)
            for k in range(4):
                lo_quarter(wq_hi_ok, 4, k, wq_hi, wq_lo, wq_ok)

            def group(i, more, more_q):
                if more:
                    split_wkv(i + 1)
                for j in range(TILES):
                    if more:
                        key_root(i + 1, j)
                        if j == 2:
                            query_root(i + 1)
                    if 3 <= j < 7:
                        lo_quarter(wo_hi_ok, i * 4, j - 3, wo_hi, wo_lo, wo_ok)
                    if 13 <= j and more_q:
                        lo_quarter(wq_hi_ok, i * 4 + 8, j - 13, wq_hi, wq_lo, wq_ok)

            with pool.Fori(0, LOOPED) as i:
                group(i, True, True)
            group(LOOPED, True, False)
            group(LOOPED + 1, False, False)

            pool.wait_ge(res_ok, HPG * GROUPS + 1)
            link(nc.gpsimd.memset(upto[:, :], 1.0))
            nc.gpsimd.affine_select(out=upto[:, :], in_=upto[:, :], compare_op=ALU.is_ge, fill=0.0, base=0,
                                    pattern=[[1, P]], channel_multiplier=-1).then_inc(const_ok, 1)
            pool.wait_ge(const_ok, 6)
            nc.gpsimd.tensor_scalar(after[:, :], upto[:, :], -1.0, 1.0, ALU.mult, ALU.add).then_inc(const_ok, 1)
            layernorm_root(2)
            pool.wait_ge(small2_in, 16 * SMALL_LOADS)
            pool.wait_ge(a_split, 2)

            def segments_lo(g):
                if g >= 2:
                    pool.wait_ge(seg_done, 2 * (g - 1))
                nc.gpsimd.tensor_tensor(seg_lo[g % 2][:, :, :],
                                        a_lo[:, g * GH:(g + 1) * GH].unsqueeze(2).broadcast_to([P, GH, P]),
                                        upto[:, :].unsqueeze(1).broadcast_to([P, GH, P]), ALU.mult).then_inc(seg_lo_ok, 1)

            def group_inputs(g):
                x3 = xs[:, g * GW:(g + 1) * GW].rearrange("p (h d) -> p h d", h=GH)
                pool.wait_ge(xs_ok, g + 1)
                if g >= 2:
                    pool.wait_ge(y_done, g - 1)
                    pool.wait_ge(y_ok, g - 1)
                nc.gpsimd.tensor_tensor(dtx[g % 2][:, :].rearrange("p (h d) -> p h d", h=GH), x3,
                                        dt[:, g * GH:(g + 1) * GH].unsqueeze(2).broadcast_to([P, GH, MP]),
                                        ALU.mult).then_inc(dtx_ok, 1)
                nc.gpsimd.tensor_tensor(xd[g % 2][:, :].rearrange("p (h d) -> p h d", h=GH), x3,
                                        dskip[:, g * GH:(g + 1) * GH].unsqueeze(2).broadcast_to([P, GH, MP]),
                                        ALU.mult).then_inc(xd_ok, 1)

            def group_root(g):
                r = slice(g, g + 1)
                pool.wait_ge(g_ms_ok, g + 1)
                link(nc.gpsimd.tensor_scalar(g_rs[:, r], g_ms[:, r], 1.0 / GW, LN_EPS, ALU.mult, ALU.add))
                nc.gpsimd.tensor_tensor(g_rs[:, r], g_rs[:, r], neghalf[:, 0:1], ALU.pow).then_inc(g_rs_ok, 1)

            def gate_lo(g, chunks):
                w = big_buffer("gate", g)
                for k in chunks:
                    pool.wait_ge(wg_hi_ok, DC * g + k + 1)
                    nc.gpsimd.tensor_tensor(wg_lo[g % 2][:, k, :], w[:, k, :], wg_hi[g % 2][:, k, :], ALU.subtract)\
                        .then_inc(wg_lo_ok, 1)

            gate_lo(0, range(DC))
            gate_lo(1, range(DC))
            for t in range(MG + 2):
                if 1 <= t <= MG:
                    group_inputs(t - 1)
                if t < MG:
                    segments_lo(t)
                if t >= 2:
                    group_root(t - 2)
                if t + 2 < MG:
                    gate_lo(t + 2, range(DC))
            layernorm_root(3)

        @block.scalar
        def _(act):
            def hi_part(dst, src, done):
                nc.scalar.activation(dst, src, ACT.Copy).then_inc(done, 1)

            def key_squares(p, j):
                act.wait_ge(kv_done, p * TILES + (j + 1))
                if not (isinstance(p, int) and j == 0):
                    act.wait_ge(k_ms_ok, p * TILES + j)
                nc.scalar.activation(junk[:, :], kv_bank(p, j)[:, 0:HD], ACT.Square, scale=HD ** -0.5,
                                     accum_out=k_ms[:, j:j + 1]).then_inc(k_ms_ok, 1)

            def values_hi(p, j):
                hi_part(v_hi[:, j, :], kv_bank(p, j)[:, HD:2 * HD], v_hi_ok)

            def keys_hi(p, b):
                t = batch_tiles(b)
                act.wait_ge(k_tp, p * KT_BATCHES + (b + 1))
                hi_part(kt_hi[:, t.start * P:t.stop * P], key_bank[:, 0:len(t) * P], kt_hi_ok)

            def queries_raw(p):
                act.wait_ge(q_done, p + 1)
                nc.scalar.activation(q_raw[:, :, :].rearrange("p h d -> p (h d)"), q_bank[:, :], ACT.Copy)\
                    .then_inc(q_raw_ok, 1)

            def queries_hi(p):
                act.wait_ge(qt_ok, p + 1)
                hi_part(qt_hi[:, :], q_tmp[:, :, :].rearrange("p h d -> p (h d)"), qt_hi_ok)

            def exps_hi(i, j, more):
                act.wait_ge(p_tp, i * TILES + (j + 1))
                slots = 2 if more else 4
                if j >= slots:
                    act.wait_ge(pv_done, i * TILES + (j - slots + 1))
                hi_part(pt(more, j)[0], exp_bank(more, j)[:, :], pt_hi_ok)

            def hi_quarter(k, hi, done):
                hi_part(hi[:, k, :], wx_raw[:, k, :], done)

            def context_hi(n):
                act.wait_ge(ctx_in[n], 16)
                hi_part(kv_hi[:, :, n * HALF:(n + 1) * HALF], probs[:, :, n * HALF:(n + 1) * HALF], ctx_hi_ok)

            act.wait_ge(wkv_in, 16)
            hi_part(wkv_hi[:, :, :], wkv_raw[:, :, :], wkv_hi_ok)
            context_hi(0)
            context_hi(1)
            for j in range(TILES):
                if j == 12:
                    queries_raw(0)
                if j == 15:
                    queries_hi(0)
                key_squares(0, j)
                values_hi(0, j)
                if j % 2 == 0 and j // 2 + 2 < HALVES:
                    context_hi(j // 2 + 2)
                if j == 3:
                    act.wait_ge(ln_tp, 1)
                    hi_part(kv_hi[:, :, CTX:KV], bank[0][:, :].rearrange("p (c n) -> p c n", c=DC), xt_hi_ok)
                if j >= 6 and (j - 6) % KT_BATCH == 0:
                    keys_hi(0, (j - 6) // KT_BATCH)
                if j in FIRST_WQ_STEPS:
                    if j == FIRST_WQ_STEPS[0]:
                        act.wait_ge(wx_in, 16)
                    hi_quarter(FIRST_WQ_STEPS.index(j), wq_hi, wq_hi_ok)
            keys_hi(0, 3)
            keys_hi(0, 4)
            act.wait_ge(wx_in, 32)
            for k in range(4):
                hi_quarter(k, wq_hi, wq_hi_ok)

            def group(i, more, more_q):
                for h in range(HPG):
                    act.wait_ge(max_ok, i * HPG + (h + 1))
                    for c in range(PARTS):
                        if c < CHUNKS:
                            src, dst = bank[(CHUNKS * h + c) % SCORE_BANKS][:, :], probs[:, h, c * CHUNK:(c + 1) * CHUNK]
                        else:
                            src, dst = key_bank[:, h * P:(h + 1) * P], probs[:, h, CTX:KV]
                        nc.scalar.activation(dst, src, ACT.Exp, bias=neg_max[:, h:h + 1],
                                             accum_out=part_sum[:, h, c:c + 1]).then_inc(exp_ok, 1)
                if more:
                    queries_raw(i + 1)
                exps_hi(i, 0, more)
                if more:
                    key_squares(i + 1, 0)
                for j in range(TILES):
                    if j + 1 < TILES:
                        exps_hi(i, j + 1, more)
                        if more:
                            key_squares(i + 1, j + 1)
                    if more or j + 1 == TILES:
                        act.wait_ge(pv_done, i * TILES + (j + 1))
                    if j + 1 == TILES:
                        hi_part(o_hi[:, :], out_bank[:, :], o_hi_ok)
                    if more:
                        if j >= 1:
                            act.wait_ge(kn_ok, i * TILES + (TILES + j + 1))
                        if j + 1 == TILES:
                            keys_hi(i + 1, 4)
                        values_hi(i + 1, j)
                        if j == 7:
                            queries_hi(i + 1)
                        if j in (5, 9, 13, 15):
                            keys_hi(i + 1, 3 if j == 15 else (j - 5) // KT_BATCH)
                    if 1 <= j <= 4:
                        if j == 1:
                            act.wait_ge(wx_in, i * 32 + (48 if more else 32))
                            act.wait_ge(wo_done, i * HPG + 1)
                        hi_quarter(j - 1, wo_hi, wo_hi_ok)
                    if more_q and 11 <= j <= 14:
                        if j == 11:
                            act.wait_ge(wx_in, i * 32 + 64)
                            act.wait_ge(q_done, i + 2)
                        hi_quarter(j - 11, wq_hi, wq_hi_ok)

            with act.Fori(0, LOOPED) as i:
                group(i, True, True)
            group(LOOPED, True, False)
            group(LOOPED + 1, False, False)

            act.wait_ge(small2_in, 16 * SMALL_LOADS)
            act.wait_ge(res_ok, HPG * GROUPS + 1)
            nc.scalar.activation(neg_a[:, :], alog[:, :], ACT.Exp).then_inc(sp_act, 1)
            act.wait_ge(ln_tp, 2)
            nc.scalar.activation(xnt[:, :, :].rearrange("p c n -> p (c n)"), bank[0][:, :], ACT.Copy).then_inc(xnt_ok, 1)
            hi_part(xnt_hi[:, :, :].rearrange("p c n -> p (c n)"), bank[0][:, :], xnt_hi_ok)
            act.wait_ge(sp_dve, 2)
            nc.scalar.activation(sp_t[:, 2, :], sp_t[:, 1, :], ACT.Exp).then_inc(sp_act, 1)
            act.wait_ge(sp_dve, 3)
            nc.scalar.activation(sp_t[:, 4, :], sp_t[:, 3, :], ACT.Ln).then_inc(sp_act, 1)

            def last_tap(c):
                act.wait_ge(blk_done, blocks_to("bc", c) if c < BC_BLKS else blocks_to("x", c - BC_BLKS))
                if c >= 2:
                    act.wait_ge(conv_ok, c - 1)
                for t in range(TPB):
                    k = conv_tile(c, t)
                    last = nc.scalar.activation(cacc[c % 2][:, t, :], conv_bank(c)[:, t * P:(t + 1) * P], ACT.Identity,
                                                scale=cw[:, k, TAPS - 1:TAPS], bias=cb[:, k:k + 1])
                last.then_inc(tap0_ok, 1)

            def conv_silu(c):
                act.wait_ge(taps_ok, c + 1)
                if c < BC_BLKS:
                    dst = bc_t[:, TPB * c:TPB * (c + 1), :]
                else:
                    g = c - BC_BLKS
                    if g >= 2:
                        act.wait_ge(x_tp, g - 1)
                    dst = xc_t[g % 2][:, :, :]
                nc.scalar.activation(dst, cacc[c % 2][:, :, :], ACT.Silu).then_inc(conv_ok, 1)

            def gate_hi(g):
                m = BIG.index(("gate", g))
                act.wait_ge(w_in_in[m % 8], 16 * (m // 8 + 1))
                if g >= 2:
                    act.wait_ge(blk_done, blocks_to("gate", g - 2))
                for k in range(DC):
                    hi_part(wg_hi[g % 2][:, k, :], w_in[m % 8][:, k, :], wg_hi_ok)

            def gate_silu(g):
                act.wait_ge(blk_done, blocks_to("gate", g))
                if g >= 2:
                    act.wait_ge(gatew_ok, g - 1)
                nc.scalar.activation(sg[g % 2][:, :], bank[3][:, :], ACT.Silu).then_inc(gate_ok, 1)

            gate_hi(0)
            last_tap(0)
            for c in range(1, BC_BLKS):
                last_tap(c)
                conv_silu(c - 1)
                if c == 1:
                    gate_hi(1)
            for t in range(MG + 3):
                if t < MG:
                    last_tap(BC_BLKS + t)
                    if t == 0:
                        conv_silu(BC_BLKS - 1)
                if 1 <= t <= MG:
                    g = t - 1
                    for half in range(2):
                        act.wait_ge(seg_done, 2 * g + half + 1)
                        if g >= 2 and half == 0:
                            act.wait_ge(y_done, g - 1)
                        nc.scalar.activation(dec[g % 2][:, 4 * half:4 * half + 4, :].rearrange("p h n -> p (h n)"),
                                             bank[half][:, :], ACT.Exp).then_inc(dec_ok, 1)
                    act.wait_ge(x_tp, g + 1)
                    nc.scalar.activation(xs[:, g * BLK:(g + 1) * BLK], bank[4][:, :], ACT.Copy).then_inc(xs_ok, 1)
                if t >= 3:
                    g = t - 3
                    act.wait_ge(y_tp, g + 1)
                    if g >= 2:
                        act.wait_ge(op_done, g - 1)
                    nc.scalar.activation(yt[g % 2][:, :, :].rearrange("p c n -> p (c n)"), bank[5][:, :], ACT.Copy)\
                        .then_inc(yt_ok, 1)
                if t == 0:
                    gate_silu(t)
                    gate_hi(t + 2)
                    conv_silu(BC_BLKS + t)
                elif t < MG:
                    conv_silu(BC_BLKS + t)
                    gate_silu(t)
                if 2 <= t < MG + 2:
                    g = t - 2
                    act.wait_ge(y_ok, g + 1)
                    nc.scalar.activation(sq[:, :], y[g % 2][:, :], ACT.Square, accum_out=g_ms[:, g:g + 1])\
                        .then_inc(g_ms_ok, 1)
                if 1 <= t < MG - 2:
                    gate_hi(t + 2)
            act.wait_ge(ln_tp, 3)
            nc.scalar.activation(xnt[:, :, :].rearrange("p c n -> p (c n)"), bank[0][:, :], ACT.Copy).then_inc(xnt_ok, 1)

        @block.vector
        def _(dve):
            steps = [0]

            def link(ins):
                steps[0] += 1
                ins.then_inc(dve_step, 1)
                dve.wait_ge(dve_step, steps[0])

            def lo_part(dst, src, hi, done):
                nc.vector.tensor_tensor(dst, src, hi, ALU.subtract).then_inc(done, 1)

            def layernorm(n):
                link(nc.vector.bn_stats(stats[:, :], res[:, :]))
                link(nc.vector.bn_aggr(mv[:, :], stats[:, :]))
                nc.vector.tensor_scalar(mv[:, 1:2], mv[:, 1:2], LN_EPS, None, ALU.add).then_inc(ln_var, 1)
                dve.wait_ge(ln_rs, n)
                nc.vector.tensor_scalar(xn[:, :], res[:, :], mv[:, 0:1], rstd[:, 0:1], ALU.subtract, ALU.mult)\
                    .then_inc(ln_out, 1)

            def keys_normed(p, j):
                dve.wait_ge(k_rs_ok, p * (2 * TILES) + (2 * j + 2))
                if j >= KN_SLOTS:
                    dve.wait_ge(k_tp, p * KT_BATCHES + (j // KT_BATCH - 1))
                nc.vector.tensor_scalar(kn[:, j % KN_SLOTS, :], kv_bank(p, j)[:, 0:HD], k_rs[:, j:j + 1], None, ALU.mult)\
                    .then_inc(kn_ok, 1)

            def values_lo(p, j):
                dve.wait_ge(v_hi_ok, p * TILES + (j + 1))
                lo_part(v_lo[:, j, :], kv_bank(p, j)[:, HD:2 * HD], v_hi[:, j, :], v_lo_ok)

            def keys_lo(p, b):
                t = batch_tiles(b)
                s = slice(t.start * P, t.stop * P)
                dve.wait_ge(kt_hi_ok, p * KT_BATCHES + (b + 1))
                lo_part(kt_lo[:, s], key_bank[:, 0:len(t) * P], kt_hi[:, s], kt_lo_ok)

            def queries_squares(p):
                dve.wait_ge(q_raw_ok, p + 1)
                nc.vector.tensor_tensor(q_tmp[:, :, :], q_raw[:, :, :], q_raw[:, :, :], ALU.mult).then_inc(q_sq_ok, 1)
                dve.wait_ge(q_sq_ok, p + 1)
                nc.vector.tensor_reduce(q_ms[:, :], q_tmp[:, :, :], AX.X, ALU.add).then_inc(q_ms_ok, 1)

            def queries_normed(p):
                dve.wait_ge(q_rs_ok, p * 3 + 3)
                nc.vector.tensor_tensor(q_tmp[:, :, :], q_raw[:, :, :], q_rs[:, :].unsqueeze(2).broadcast_to([P, HPG, HD]),
                                        ALU.mult).then_inc(qn_ok, 1)

            def queries_weighted(p):
                dve.wait_ge(q_tp, p + 1)
                nc.vector.tensor_scalar(q_tmp[:, :, :].rearrange("p h d -> p (h d)"), q_bank[:, :], qkw[:, 2:3], None,
                                        ALU.mult).then_inc(qt_ok, 1)

            def queries_lo(p):
                dve.wait_ge(qt_hi_ok, p + 1)
                lo_part(qt_lo[:, :], q_tmp[:, :, :].rearrange("p h d -> p (h d)"), qt_hi[:, :], qt_lo_ok)

            def exps_lo(i, j, more):
                hi, lo = pt(more, j)
                dve.wait_ge(pt_hi_ok, i * TILES + (j + 1))
                lo_part(lo, exp_bank(more, j)[:, :], hi, pt_lo_ok)

            dve.sem_inc(res_ok, 1)
            link(nc.vector.memset(res_odd[:, :], 0.0))
            def context_lo(n):
                s = slice(n * HALF, (n + 1) * HALF)
                dve.wait_ge(ctx_hi_ok, n + 1)
                lo_part(kv_lo[:, :, s], probs[:, :, s], kv_hi[:, :, s], ctx_lo_ok)

            dve.wait_ge(wkv_hi_ok, 1)
            lo_part(wkv_lo[:, :, :], wkv_raw[:, :, :], wkv_hi[:, :, :], wkv_ok)
            context_lo(0)
            context_lo(1)
            dve.wait_ge(x_in, 16)
            dve.wait_ge(const_ok, 5)
            layernorm(1)
            for j in range(TILES):
                if j == 12:
                    queries_squares(0)
                if j == 15:
                    queries_weighted(0)
                if j == 16:
                    queries_lo(0)
                values_lo(0, j)
                if j >= 1:
                    keys_normed(0, j - 1)
                if j % 2 == 0 and j // 2 + 2 < HALVES:
                    context_lo(j // 2 + 2)
                if j == 3:
                    dve.wait_ge(xt_hi_ok, 1)
                    lo_part(kv_lo[:, :, CTX:KV], bank[0][:, :].rearrange("p (c n) -> p c n", c=DC), kv_hi[:, :, CTX:KV],
                            xt_lo_ok)
                if j == 7:
                    dve.wait_ge(small_in, 32)
                    link(nc.vector.tensor_scalar(qkw[:, 2:3], qkw[:, 0:1], qkw[:, 1:2], float(HD) ** -0.5,
                                                 ALU.mult, ALU.mult))
                if j >= 6 and (j - 6) % KT_BATCH == 0:
                    keys_lo(0, (j - 6) // KT_BATCH)
                if j == 13:
                    queries_normed(0)
            keys_normed(0, TILES - 1)
            keys_lo(0, 3)

            def chunk_maximum(i, n):
                dve.wait_ge(scores, i * N_SC + (SCORE_ORDER.index(n) + 1))
                nc.vector.tensor_reduce(part_max[:, n // CHUNKS, n % CHUNKS:n % CHUNKS + 1], bank[n % SCORE_BANKS][:, :],
                                        AX.X, ALU.max).then_inc(part_max_ok, 1)

            def latents_maxima(i):
                dve.wait_ge(last_scores, i + 1)
                nc.vector.tensor_reduce(part_max[:, :, CHUNKS], key_bank[:, :].rearrange("p (h n) -> p h n", h=HPG),
                                        AX.X, ALU.max).then_inc(part_max_ok, 1)

            def head_maximum(i, h):
                dve.wait_ge(part_max_ok, i * (N_SC + 1) + (CHUNKS * (h + 1) + 1))
                nc.vector.tensor_reduce(neg_max[:, h:h + 1], part_max[:, h, :], AX.X, ALU.max, negate=True)\
                    .then_inc(max_ok, 1)

            for n in SCORE_ORDER[:3]:
                chunk_maximum(0, n)
            keys_lo(0, 4)
            chunk_maximum(0, SCORE_ORDER[3])
            latents_maxima(0)
            head_maximum(0, 0)
            chunk_maximum(0, EARLY - 1)

            def group(i, more):
                for h in range(1, HPG):
                    for n in range(max(CHUNKS * h, EARLY), CHUNKS * (h + 1)):
                        chunk_maximum(i, n)
                    head_maximum(i, h)
                exps_lo(i, 0, more)
                for j in range(TILES):
                    if j + 1 < TILES:
                        exps_lo(i, j + 1, more)
                    if j == 2:
                        dve.wait_ge(exp_ok, i * N_EX + N_EX)
                        nc.vector.tensor_reduce(row_sum[:, :], part_sum[:, :, :], AX.X, ALU.add).then_inc(sum_ok, 1)
                        dve.wait_ge(sum_ok, i + 1)
                        nc.vector.reciprocal(inv_sum[:, :], row_sum[:, :]).then_inc(inv_ok, 1)
                    if j + 1 == TILES:
                        if more:
                            keys_normed(i + 1, j)
                            for n in SCORE_ORDER[:2]:
                                chunk_maximum(i + 1, n)
                            keys_lo(i + 1, 4)
                        dve.wait_ge(o_hi_ok, i + 1)
                        lo_part(o_lo[:, :], out_bank[:, :], o_hi[:, :], o_lo_ok)
                    if more:
                        values_lo(i + 1, j)
                        if j == 0:
                            keys_normed(i + 1, 0)
                        if j + 1 < TILES - 1:
                            keys_normed(i + 1, j + 1)
                        if j == 1:
                            queries_squares(i + 1)
                        if j == 3:
                            queries_normed(i + 1)
                        if j == 6:
                            queries_weighted(i + 1)
                        if j == 8:
                            queries_lo(i + 1)
                        if j in (5, 9, 13, 15):
                            keys_lo(i + 1, 3 if j == 15 else (j - 5) // KT_BATCH)
                if more:
                    chunk_maximum(i + 1, SCORE_ORDER[2])
                    chunk_maximum(i + 1, SCORE_ORDER[3])
                    latents_maxima(i + 1)
                    head_maximum(i + 1, 0)
                for h in range(HPG):
                    to = (res, res_odd)[h % 2]
                    dve.wait_ge(wo_done, i * HPG + (h + 2))
                    dve.wait_ge(res_ok, i * HPG + h)
                    if h == 0:
                        dve.wait_ge(inv_ok, i + 1)
                    nc.vector.scalar_tensor_tensor(out=to[:, :], in0=wo_bank(h)[:, :], scalar=inv_sum[:, h:h + 1],
                                                   in1=to[:, :], op0=ALU.mult, op1=ALU.add).then_inc(res_ok, 1)
                if more:
                    chunk_maximum(i + 1, EARLY - 1)

            with dve.Fori(0, LOOPED) as i:
                group(i, True)
            group(LOOPED, True)
            group(LOOPED + 1, False)

            dve.wait_ge(res_ok, HPG * GROUPS + 1)
            link(nc.vector.tensor_tensor(res[:, :], res[:, :], res_odd[:, :], ALU.add))
            layernorm(2)
            dve.wait_ge(small2_in, 16 * SMALL_LOADS)
            dve.wait_ge(dt_done, 1)
            X, NA, E, U, L, T = (sp_t[:, k, :] for k in range(6))
            nc.vector.tensor_tensor(X, bank[1][:, 0:MH], dtb[:, :], ALU.add).then_inc(sp_dve, 1)
            dve.wait_ge(sp_dve, 1)
            nc.vector.scalar_tensor_tensor(out=NA, in0=X, scalar=-1.0, in1=X, op0=ALU.mult, op1=ALU.min).then_inc(sp_dve, 1)
            dve.wait_ge(sp_act, 2)
            nc.vector.tensor_scalar(U, E, 1.0, None, ALU.add).then_inc(sp_dve, 1)
            dve.wait_ge(sp_dve, 3)
            link(nc.vector.tensor_scalar(T, U, -1.0, None, ALU.add))
            link(nc.vector.tensor_scalar(NA, T, 0.0, None, ALU.is_equal))
            link(nc.vector.tensor_tensor(T, T, NA, ALU.add))
            link(nc.vector.reciprocal(T, T))
            link(nc.vector.tensor_tensor(T, T, E, ALU.mult))
            dve.wait_ge(sp_act, 3)
            link(nc.vector.tensor_tensor(T, T, L, ALU.mult))
            link(nc.vector.tensor_tensor(NA, NA, E, ALU.mult))
            link(nc.vector.tensor_tensor(T, T, NA, ALU.add))
            nc.vector.scalar_tensor_tensor(out=dt[:, :], in0=X, scalar=zero1[:, 0:1], in1=T, op0=ALU.max, op1=ALU.add)\
                .then_inc(dt_ok, 1)
            dve.wait_ge(dt_ok, 1)
            nc.vector.scalar_tensor_tensor(out=a_dt[:, :], in0=dt[:, :], scalar=-1.0, in1=neg_a[:, :],
                                           op0=ALU.mult, op1=ALU.mult).then_inc(dt_ok, 1)
            dve.wait_ge(dt_ok, 2)
            nc.vector.tensor_copy(a_hi[:, :], a_dt[:, :]).then_inc(a_split, 1)
            dve.wait_ge(a_split, 1)
            lo_part(a_lo[:, :], a_dt[:, :], a_hi[:, :], a_split)

            def other_taps(c):
                dve.wait_ge(tap0_ok, c + 1)
                for back in range(1, TAPS):
                    for t in range(TPB):
                        k = conv_tile(c, t)
                        last = nc.vector.scalar_tensor_tensor(
                            out=cacc[c % 2][:, t, back:Q], in0=conv_bank(c)[:, t * P:(t + 1) * P - back],
                            scalar=cw[:, k, TAPS - 1 - back:TAPS - back], in1=cacc[c % 2][:, t, back:Q],
                            op0=ALU.mult, op1=ALU.add)
                    if back + 1 < TAPS:
                        link(last)
                last.then_inc(taps_ok, 1)

            def segments_hi(g):
                if g >= 2:
                    dve.wait_ge(seg_done, 2 * (g - 1))
                nc.vector.tensor_tensor(seg_hi[g % 2][:, :, :],
                                        a_hi[:, g * GH:(g + 1) * GH].unsqueeze(2).broadcast_to([P, GH, P]),
                                        upto[:, :].unsqueeze(1).broadcast_to([P, GH, P]), ALU.mult).then_inc(seg_ok, 1)

            dve.wait_ge(xnt_hi_ok, 1)
            flat = "p c n -> p (c n)"
            lo_part(xnt_lo[:, :, :].rearrange(flat), bank[0][:, :], xnt_hi[:, :, :].rearrange(flat), xnt_lo_ok)
            for c in range(BC_BLKS):
                other_taps(c)
            dve.wait_ge(const_ok, 7)
            for t in range(MG + 2):
                if t < MG:
                    other_taps(BC_BLKS + t)
                    segments_hi(t)
                if t == 0:
                    for half in range(2):
                        dve.wait_ge(cb_done, half + 1)
                        nc.vector.tensor_tensor(gm[:, 4 * half:4 * half + 4, :],
                                                bank[4 + half][:, :].rearrange("p (g n) -> p g n", g=4),
                                                upto[:, :].unsqueeze(1).broadcast_to([P, 4, P]), ALU.mult).then_inc(gm_ok, 1)
                if 1 <= t <= MG:
                    g = t - 1
                    dve.wait_ge(gm_ok, 2)
                    for half in range(2):
                        h = slice(4 * half, 4 * half + 4)
                        dve.wait_ge(dec_ok, 2 * g + half + 1)
                        nc.vector.tensor_tensor(dec[g % 2][:, h, :], dec[g % 2][:, h, :],
                                                gm[:, g:g + 1, :].broadcast_to([P, 4, P]), ALU.mult)\
                            .then_inc(mix_ok, 1)
                if t < MG:
                    s = slice(t * BLK, (t + 1) * BLK)
                    if t == 0:
                        dve.wait_ge(norm_in, 16)
                    dve.wait_ge(gate_ok, t + 1)
                    nc.vector.tensor_tensor(gate[:, s], gate[:, s], sg[t % 2][:, :], ALU.mult).then_inc(gatew_ok, 1)
                if t >= 2:
                    g = t - 2
                    dve.wait_ge(y_done, g + 1)
                    dve.wait_ge(xd_ok, g + 1)
                    if g >= 2:
                        dve.wait_ge(y_tp, g - 1)
                    nc.vector.tensor_tensor(y[g % 2][:, :], bank[6][:, :], xd[g % 2][:, :], ALU.add).then_inc(y_ok, 1)
                    dve.wait_ge(g_rs_ok, g + 1)
                    dve.wait_ge(gatew_ok, g + 1)
                    nc.vector.scalar_tensor_tensor(out=y[g % 2][:, :], in0=y[g % 2][:, :], scalar=g_rs[:, g:g + 1],
                                                   in1=gate[:, g * GW:(g + 1) * GW], op0=ALU.mult, op1=ALU.mult)\
                        .then_inc(yn_ok, 1)
            dve.wait_ge(op_done, MG)
            nc.vector.tensor_tensor(res[:, :], res[:, :], bank[7][:, :], ALU.add).then_inc(res_final, 1)
            dve.wait_ge(res_final, 1)
            layernorm(3)

            dve.wait_ge(ffn_in, 16 * FFN_LOADS)
            link(nc.vector.tensor_copy(lstf[:, :], lst[:, :]))
            link(nc.vector.tensor_scalar(lmask[:, :], lstf[:, :], 0.0, None, ALU.is_le))
            link(nc.vector.tensor_reduce(lcnt[:, :], lmask[:, :], AX.X, ALU.add))
            link(nc.vector.tensor_tensor(lmask[:, 0:1], lcnt[:, :], lrow[:, :], ALU.is_equal))
            link(nc.vector.tensor_tensor(res[:, :], res[:, :], lbias[:, :], ALU.add))
            dve.wait_ge(la_done, 1)
            nc.vector.tensor_scalar(lt[:, :], bank[1][0:AR, 0:Q], lmask[:, 0:1], None, ALU.mult).then_inc(lt_ok, 1)
            dve.wait_ge(ffn_done, 1)
            nc.vector.tensor_tensor(fin[:, :], bank[2][:, :], res[:, :], ALU.add).then_inc(fin_ok, 1)

        @block.tensor
        def _(pe):
            def split_product(dst, a_hi, a_lo, b_hi, b_lo, start, stop):
                nc.tensor.matmul(dst, a_hi, b_hi, start=start, stop=False)
                nc.tensor.matmul(dst, a_hi, b_lo, start=False, stop=False)
                return nc.tensor.matmul(dst, a_lo, b_hi, start=False, stop=stop)

            def keep_clock(n):
                for _ in range(n):
                    nc.tensor.matmul(bank[7][:, 0:P], ident[:, :], ident[:, :], start=True, stop=True)

            def rows_transposed(n):
                pe.wait_ge(ln_out, n)
                for c in range(DC):
                    last = nc.tensor.transpose(bank[0][:, c * P:(c + 1) * P], xn[:, c * P:(c + 1) * P], ident[:, :])
                last.then_inc(ln_tp, 1)

            def queries():
                for c in range(DC):
                    last = split_product(q_bank[:, :], kv_hi[:, c, CTX:KV], kv_lo[:, c, CTX:KV], wq_hi[:, c, :], wq_lo[:, c, :],
                                         c == 0, c == DC - 1)
                last.then_inc(q_done, 1)

            def queries_transposed(p):
                pe.wait_ge(qn_ok, p + 1)
                for h in range(HPG):
                    last = nc.tensor.transpose(q_bank[:, h * P:(h + 1) * P], q_tmp[:, h, :], ident[:, :])
                last.then_inc(q_tp, 1)

            def keys_values(p, j):
                banks = 5 if isinstance(p, int) and p == 0 else 3
                if j >= banks:
                    pe.wait_ge(v_lo_ok, p * TILES + (j - banks + 1))
                    pe.wait_ge(kn_ok, p * TILES + (j - banks + 1))
                t = slice(j * P, (j + 1) * P)
                for c in range(DC):
                    last = split_product(kv_bank(p, j)[:, 0:2 * HD], kv_hi[:, c, t], kv_lo[:, c, t], wkv_hi[:, c, :], wkv_lo[:, c, :],
                                         c == 0, c == DC - 1)
                last.then_inc(kv_done, 1)

            def keys_transposed(p, b):
                t = batch_tiles(b)
                pe.wait_ge(kn_ok, p * TILES + t.stop)
                if b >= 1:
                    pe.wait_ge(kt_lo_ok, p * KT_BATCHES + b)
                for k, j in enumerate(t):
                    last = nc.tensor.transpose(key_bank[:, k * P:(k + 1) * P], kn[:, j % KN_SLOTS, :], ident[:, :])
                last.then_inc(k_tp, 1)

            pe.sem_inc(wo_done, 1)
            pe.wait_ge(const_ok, 5)
            keep_clock(CLOCK_FILL[0])
            for j in range(TILES):
                if j == 0:
                    pe.wait_ge(wkv_ok, 1)
                if j == 3:
                    rows_transposed(1)
                if j < CTX // P and j % 2 == 0:
                    pe.wait_ge(ctx_lo_ok, j // 2 + 1)
                if j == 12:
                    pe.wait_ge(wq_ok, 1)
                    pe.wait_ge(xt_lo_ok, 1)
                    queries()
                if j == 15:
                    queries_transposed(0)
                keys_values(0, j)
                if j >= 6 and (j - 6) % KT_BATCH == 0:
                    keys_transposed(0, (j - 6) // KT_BATCH)
            def chunk_scores(i, n):
                h, c = n // CHUNKS, n % CHUNKS
                s, k = slice(h * P, (h + 1) * P), slice(c * CHUNK, (c + 1) * CHUNK)
                split_product(bank[n % SCORE_BANKS][:, :], qt_hi[:, s], qt_lo[:, s], kt_hi[:, k], kt_lo[:, k], True, True)\
                    .then_inc(scores, 1)

            def latents_scores(p):
                pe.wait_ge(kt_lo_ok, p * KT_BATCHES + KT_BATCHES)
                for h in range(HPG):
                    s = slice(h * P, (h + 1) * P)
                    last = split_product(key_bank[:, s], qt_hi[:, s], qt_lo[:, s], kt_hi[:, CTX:KV], kt_lo[:, CTX:KV], True, True)
                last.then_inc(last_scores, 1)

            pe.wait_ge(qt_lo_ok, 1)
            pe.wait_ge(kt_lo_ok, 2)
            pe.wait_ge(v_lo_ok, TILES - 3)
            chunk_scores(0, SCORE_ORDER[0])
            keys_transposed(0, 3)
            chunk_scores(0, SCORE_ORDER[1])
            chunk_scores(0, SCORE_ORDER[2])
            keys_transposed(0, 4)
            pe.wait_ge(v_lo_ok, TILES)
            chunk_scores(0, SCORE_ORDER[3])
            latents_scores(0)
            chunk_scores(0, EARLY - 1)

            def group(i, more):
                def exps_transposed(j):
                    if j == 0:
                        pe.wait_ge(exp_ok, i * N_EX + exps_before(14 if more else 12))
                    elif j == 1:
                        if more:
                            pe.wait_ge(exp_ok, i * N_EX + exps_before(15))
                    elif j == (2 if more else 4):
                        pe.wait_ge(exp_ok, i * N_EX + N_EX)
                    slots = 2 if more else 4
                    if j >= slots:
                        pe.wait_ge(pt_lo_ok, i * TILES + (j - slots + 1))
                    for h in range(HPG):
                        last = nc.tensor.transpose(exp_bank(more, j)[:, h * P:(h + 1) * P],
                                                   probs[:, h, j * P:(j + 1) * P], ident[:, :])
                    last.then_inc(p_tp, 1)

                for n in range(EARLY, N_SC):
                    if n == 5:
                        pe.wait_ge(res_ok, i * HPG)
                    elif n == 6:
                        pe.wait_ge(res_ok, i * HPG + 1)
                    elif n >= SCORE_BANKS:
                        pe.wait_ge(exp_ok, i * N_EX + exps_before(n - SCORE_BANKS))
                    chunk_scores(i, n)
                if more:
                    pe.wait_ge(wq_ok, i + 2)
                    pe.wait_ge(exp_ok, i * N_EX + exps_before(9))
                    queries()
                    pe.wait_ge(wkv_ok, i + 2)
                    pe.wait_ge(exp_ok, i * N_EX + exps_before(10))
                    keys_values(i + 1, 0)
                    pe.wait_ge(exp_ok, i * N_EX + exps_before(11))
                    keys_values(i + 1, 1)
                exps_transposed(0)
                exps_transposed(1)
                if more:
                    keys_values(i + 1, 2)
                else:
                    exps_transposed(2)
                ahead = 1 if more else 3
                for j in range(TILES):
                    if (j >= 1 or not more) and j + ahead < TILES:
                        exps_transposed(j + ahead)
                    if more and j in (5, 9, 13):
                        keys_transposed(i + 1, (j - 5) // KT_BATCH)
                    if more and j == 5:
                        queries_transposed(i + 1)
                    if more and j == TILES - 1:
                        keys_transposed(i + 1, 3)
                        pe.wait_ge(qt_lo_ok, i + 2)
                        for n in SCORE_ORDER[:2]:
                            chunk_scores(i + 1, n)
                    pe.wait_ge(pt_lo_ok, i * TILES + (j + 1))
                    split_product(out_bank[:, :], v_hi[:, j, :], v_lo[:, j, :], *pt(more, j),
                                  j == 0, j == TILES - 1).then_inc(pv_done, 1)
                    if more and 1 <= j < TILES - 2:
                        keys_values(i + 1, j + 2)
                if more:
                    chunk_scores(i + 1, SCORE_ORDER[2])
                    keys_transposed(i + 1, 4)
                    pe.wait_ge(v_lo_ok, i * TILES + (2 * TILES - 1))
                    pe.wait_ge(kn_ok, i * TILES + (2 * TILES - 1))
                    chunk_scores(i + 1, SCORE_ORDER[3])
                    latents_scores(i + 1)
                pe.wait_ge(wo_ok, i + 1)
                pe.wait_ge(o_lo_ok, i + 1)
                for h in range(HPG):
                    s = slice(h * P, (h + 1) * P)
                    if h == 2 and more:
                        pe.wait_ge(v_lo_ok, i * TILES + 2 * TILES)
                        chunk_scores(i + 1, EARLY - 1)
                    if h >= 2:
                        pe.wait_ge(res_ok, i * HPG + h)
                    split_product(wo_bank(h)[:, :], o_hi[:, s], o_lo[:, s], wo_hi[:, h, :], wo_lo[:, h, :], True, True)\
                        .then_inc(wo_done, 1)

            with pe.Fori(0, LOOPED) as i:
                group(i, True)
            group(LOOPED, True)
            group(LOOPED + 1, False)

            def product(dst, lhs, rhs):
                for c in range(DC):
                    last = nc.tensor.matmul(dst, lhs(c), rhs(c), start=c == 0, stop=c == DC - 1)
                return last

            keep_clock(CLOCK_FILL[1])
            rows_transposed(2)
            pe.wait_ge(xnt_ok, 1)
            pe.wait_ge(small2_in, 16 * SMALL_LOADS)
            product(bank[1][:, 0:MH], lambda c: xnt[:, c, :], lambda c: wdt[:, c, :]).then_inc(dt_done, 1)

            def big(kind, k):
                m = BIG.index((kind, k))
                pe.wait_ge(w_in_in[m % 8], 16 * (m // 8 + 1))
                return w_in[m % 8]

            def conv_block(c):
                w = big("bc", c) if c < BC_BLKS else big("x", c - BC_BLKS)
                if c == BC_BLKS - 1:
                    pe.wait_ge(xnt_lo_ok, 1)
                if c == BC_BLKS:
                    pe.wait_ge(taps_ok, 1)
                elif c == BC_BLKS + 2:
                    pe.wait_ge(taps_ok, BC_BLKS + 1)
                elif c > BC_BLKS + 2:
                    pe.wait_ge(taps_ok, c)
                for t in range(TPB):
                    s = slice(t * P, (t + 1) * P)
                    last = product(conv_bank(c)[:, s], lambda k: w[:, k, s], lambda k: xnt[:, k, :])
                last.then_inc(blk_done, 1)

            def outputs_transposed(g):
                pe.wait_ge(yn_ok, g + 1)
                if g >= 1:
                    pe.wait_ge(yt_ok, g)
                for k in range(TPB):
                    s = slice(k * P, (k + 1) * P)
                    last = nc.tensor.transpose(bank[5][:, s], y[g % 2][:, s], ident[:, :])
                last.then_inc(y_tp, 1)

            def out_products(g, chunks):
                w = big("out", g)
                pe.wait_ge(yt_ok, g + 1)
                for k in chunks:
                    last = nc.tensor.matmul(bank[7][:, :], yt[g % 2][:, k, :], w[:, k, :],
                                            start=g == 0 and k == 0, stop=g == MG - 1 and k == TPB - 1)
                if chunks[-1] == TPB - 1:
                    last.then_inc(op_done, 1)

            for c in range(BC_BLKS):
                conv_block(c)
            for t in range(MG + 2):
                if t < MG:
                    conv_block(BC_BLKS + t)
                if t == 1:
                    pe.wait_ge(conv_ok, BC_BLKS)
                    for g in range(MG):
                        last = nc.tensor.matmul(bank[4 + g // 4][:, g % 4 * P:(g % 4 + 1) * P], bc_t[:, g, :],
                                                bc_t[:, MG + g, :], start=True, stop=True)
                        if g % 4 == 3:
                            last.then_inc(cb_done, 1)
                if 1 <= t <= MG:
                    g = t - 1
                    pe.wait_ge(seg_ok, g + 1)
                    pe.wait_ge(seg_lo_ok, g + 1)
                    if g == 0:
                        pe.wait_ge(const_ok, 7)
                        pe.wait_ge(taps_ok, BC_BLKS)
                        pe.wait_ge(sp_dve, 1)
                    for half in range(2):
                        if g >= 1:
                            pe.wait_ge(dec_ok, 2 * (g - 1) + half + 1)
                        h = slice(4 * half, 4 * half + 4)
                        nc.tensor.matmul(bank[half][:, :], after[:, :], seg_hi[g % 2][:, h, :].rearrange("p h n -> p (h n)"),
                                         start=True, stop=False)
                        nc.tensor.matmul(bank[half][:, :], after[:, :], seg_lo[g % 2][:, h, :].rearrange("p h n -> p (h n)"),
                                         start=False, stop=True).then_inc(seg_done, 1)
                    pe.wait_ge(conv_ok, BC_BLKS + g + 1)
                    if g == 0:
                        pe.wait_ge(gm_ok, 2)
                    else:
                        pe.wait_ge(xs_ok, g)
                    for k in range(TPB):
                        last = nc.tensor.transpose(bank[4][:, k * P:(k + 1) * P], xc_t[g % 2][:, k, :], ident[:, :])
                    last.then_inc(x_tp, 1)
                if 3 <= t <= MG + 1:
                    outputs_transposed(t - 3)
                if t < MG:
                    if t == 0:
                        pe.wait_ge(taps_ok, 2)
                    else:
                        pe.wait_ge(gate_ok, t)
                    for k in range(DC):
                        pe.wait_ge(wg_lo_ok, DC * t + k + 1)
                        last = split_product(bank[3][:, :], xnt_hi[:, k, :], xnt_lo[:, k, :], wg_hi[t % 2][:, k, :], wg_lo[t % 2][:, k, :],
                                             k == 0, k == DC - 1)
                    last.then_inc(blk_done, 1)
                if 2 <= t < MG + 2:
                    g = t - 2
                    pe.wait_ge(mix_ok, 2 * g + 2)
                    pe.wait_ge(dtx_ok, g + 1)
                    if g >= 1:
                        pe.wait_ge(y_ok, g)
                    for h in range(GH):
                        s = slice(h * MP, (h + 1) * MP)
                        last = nc.tensor.matmul(bank[6][:, s], dec[g % 2][:, h, :], dtx[g % 2][:, s], start=True, stop=True)
                    last.then_inc(y_done, 1)
                if 3 <= t <= MG:
                    out_products(t - 3, range(TPB))
            out_products(MG - 2, range(TPB - 1))
            outputs_transposed(MG - 1)
            out_products(MG - 2, range(TPB - 1, TPB))
            out_products(MG - 1, range(TPB))

            pe.wait_ge(res_final, 1)
            keep_clock(CLOCK_FILL[2])
            rows_transposed(3)
            pe.wait_ge(xnt_ok, 2)
            pe.wait_ge(ffn_in, 16 * FFN_LOADS)
            product(bank[1][0:AR, 0:Q], lambda c: la[:, c, :], lambda c: xnt[:, c, :]).then_inc(la_done, 1)
            w = big("linear", 0)
            for c in range(DC):
                nc.tensor.matmul(bank[2][:, :], xnt[:, c, :], w[:, c, :], start=c == 0, stop=False)
            pe.wait_ge(lt_ok, 1)
            nc.tensor.matmul(bank[2][:, :], lt[:, :], lb[:, :], start=False, stop=True).then_inc(ffn_done, 1)


def kernel(**inputs):
    from concourse import bacc
    from concourse.bass_utils import run_bass_kernel_spmd

    def a(name):
        return np.asarray(inputs[name])

    def chunks(m):
        return np.ascontiguousarray(m.reshape(-1, P, m.shape[1]).transpose(1, 0, 2))

    def column_blocks(m, width):
        return np.ascontiguousarray(m.reshape(m.shape[0] // P, P, -1, width).transpose(2, 1, 0, 3))

    wk, wv = (column_blocks(a(f"L0_xattn_{n}"), HD) for n in ("Wk", "Wv"))
    w_in = a("L0_attn_in_proj_w").T
    arrays = {
        "x": a("x").reshape(Q, DM),
        "ctx_t": chunks(a("ctx_4096").reshape(CTX, DM).T),
        "wq": column_blocks(a("L0_xattn_Wq"), HPG * HD),
        "wkv": np.ascontiguousarray(np.concatenate([wk, wv], axis=3)),
        "wo": np.ascontiguousarray(a("L0_xattn_Wo").reshape(GROUPS, HPG, HD, DM).transpose(0, 2, 1, 3)),
        "q_norm": a("L0_xattn_q_norm_w").reshape(HD, 1),
        "k_norm": a("L0_xattn_k_norm_w").reshape(HD, 1),
        "w_xbc": column_blocks(w_in[:, MI:MI + CONV], BLK),
        "w_gate": column_blocks(w_in[:, :MI], BLK),
        "w_dt": chunks(w_in[:, MI + CONV:]),
        "conv_w": chunks(a("L0_attn_conv_weight")),
        "conv_b": np.ascontiguousarray(a("L0_attn_conv_bias").reshape(XBC_TILES, P).T),
        "dt_bias": a("L0_attn_dt_bias").reshape(1, MH),
        "a_log": a("L0_attn_A_log").reshape(1, MH),
        "d_skip": a("L0_attn_D").reshape(1, MH),
        "norm_w": a("L0_attn_norm_weight").reshape(1, MI),
        "w_out": np.ascontiguousarray(a("L0_attn_out_proj_w").T.reshape(MG, TPB, P, DM).transpose(0, 2, 1, 3)),
        "ffn_w": chunks(a("L0_ffn_weight").T),
        "ffn_b": a("L0_ffn_bias").reshape(1, DM),
        "lora_a": chunks(a("L0_ffn_lora_A").reshape(AR, DM).T),
        "lora_b": np.ascontiguousarray(a("L0_ffn_lora_B").transpose(0, 2, 1).reshape(AR, DM)),
        "starts": a("L0_ffn_lora_start_indices").reshape(1, 4),
        "picks": np.repeat(np.arange(ADAPTERS, dtype=np.float32) + 2, RANK).reshape(AR, 1),
    }
    nc = bacc.Bacc("TRN2", target_bir_lowering=False, num_devices=1, dynamic_dma_scratch_size=1024)
    args, given = [], {}
    for name, v in arrays.items():
        given[f"in_{name}"] = np.ascontiguousarray(v)
        args.append(nc.dram_tensor(f"in_{name}", v.shape, mybir.dt.from_np(v.dtype), kind="ExternalInput").ap())
    args.append(nc.dram_tensor("layer_out", (Q, DM), F32, kind="ExternalOutput").ap())
    perceiver_program(nc, *args)
    r = run_bass_kernel_spmd(nc, [given], core_ids=[0])
    return r.results[0]["layer_out"].reshape(1, Q, DM)
```
